# Optimizing a Trainium2 kernel written in Bass

```python
import numpy as np
import jax
import jax.numpy as jnp

def _softmax(x, axis=-1):
    return jax.nn.softmax(x, axis=axis)
def _gelu(x):
    return jax.nn.gelu(x, approximate=True)
def _silu(x):
    return jax.nn.silu(x)
def _sigmoid(x):
    return jax.nn.sigmoid(x)
def _layernorm(x, axis=-1, eps=1e-5):
    m = jnp.mean(x, axis=axis, keepdims=True)
    v = jnp.var(x, axis=axis, keepdims=True)
    return (x - m) / jnp.sqrt(v + eps)
def _scatter_add(tgt, idx, src, axis=0):
    return tgt.at[idx].add(src)
def _segment_sum(src, seg, n):
    return jax.ops.segment_sum(src, seg, n)

kernel_name = 'mk_adj_resnorm_d4_adj_256_edd456'

def setup_inputs(seed: int = 0):
    np.random.seed(seed)
    _w = jnp.asarray
    def _rec_inputs():
        import jax
        import jax.numpy as jnp
        _gk = jax.random.key(seed)
        x = -0.000929 + 1 * jax.random.normal(jax.random.fold_in(_gk, 1), (32, 512, 256), jnp.float32)
        _a = jax.random.bernoulli(jax.random.fold_in(_gk, 2), 0.03125, (32, 512, 512))
        _a = jnp.logical_or(_a, jnp.eye(512, dtype=bool))
        _af = _a.astype(jnp.float32)
        adj = _af
        return x, adj
    x, adj = _rec_inputs()
    def _L0_gnn_setup():
        import jax, jax.numpy as jnp
        import numpy as np
        B, N = (1, 4096)
        D_IN, D_OUT, H = (256, 256, 8)
        HD = D_OUT // H
        NEG = -9000000000000000.0

        def _xavier(key, shape):
            lim = np.sqrt(6.0 / (shape[0] + shape[1])).astype(np.float32)
            return jax.random.uniform(key, shape, jnp.float32, -lim, lim)
        key = jax.random.key(seed)
        ks = jax.random.split(key, 8)
        x = jax.random.normal(ks[0], (B, N, D_IN), jnp.float32)
        adj = (jax.random.uniform(ks[1], (B, N, N)) < 0.05).astype(jnp.float32)
        idx = jnp.arange(N)
        adj = adj.at[:, idx, idx].set(1.0)
        Wq = _xavier(ks[2], (D_IN, D_OUT))
        bq = jnp.zeros((D_OUT,), jnp.float32)
        Wk = _xavier(ks[3], (D_IN, D_OUT))
        bk = jnp.zeros((D_OUT,), jnp.float32)
        Wv = _xavier(ks[4], (D_IN, D_OUT))
        bv = jnp.zeros((D_OUT,), jnp.float32)
        Wo = _xavier(ks[5], (D_OUT, D_OUT))
        bo = jnp.zeros((D_OUT,), jnp.float32)
        return dict(x=x, adj=adj, Wq=Wq, bq=bq, Wk=Wk, bk=bk, Wv=Wv, bv=bv, Wo=Wo, bo=bo)
    _L0_gnn_all = _L0_gnn_setup()
    _L0_gnn_in = {k: v for k, v in _L0_gnn_all.items() if k in ('Wq', 'bq', 'Wk', 'bk', 'Wv', 'bv', 'Wo', 'bo', )}
    del _L0_gnn_all

    def _L1_gnn_setup():
        import jax, jax.numpy as jnp
        import numpy as np
        D_IN = 256
        D_HID = 512
        key = jax.random.key(seed)
        k1, k2, k3, k4, k5, k6 = jax.random.split(key, 6)
        x = jax.random.normal(k1, (8, 4096, D_IN), dtype=jnp.float32)
        adj = jax.random.uniform(k2, (8, 4096, 4096), dtype=jnp.float32)
        s1 = 1.0 / np.sqrt(D_IN)
        s2 = 1.0 / np.sqrt(D_HID)
        W1 = jax.random.uniform(k3, (D_IN, D_HID), dtype=jnp.float32, minval=-s1, maxval=s1)
        b1 = jax.random.uniform(k4, (D_HID,), dtype=jnp.float32, minval=-s1, maxval=s1)
        W2 = jax.random.uniform(k5, (D_HID, D_IN), dtype=jnp.float32, minval=-s2, maxval=s2)
        b2 = jax.random.uniform(k6, (D_IN,), dtype=jnp.float32, minval=-s2, maxval=s2)
        eps = jnp.zeros((1,), dtype=jnp.float32)
        return {'x': x, 'adj': adj, 'eps': eps, 'W1': W1, 'b1': b1, 'W2': W2, 'b2': b2}
    _L1_gnn_all = _L1_gnn_setup()
    _L1_gnn_in = {k: v for k, v in _L1_gnn_all.items() if k in ('eps', 'W1', 'b1', 'W2', 'b2', )}
    del _L1_gnn_all

    def _L2_gnn_setup():
        import jax, jax.numpy as jnp
        import numpy as np
        B, N, D, H = (8, 2048, 256, 1024)
        RMS_EPS = 1e-06

        def _rmsnorm(h, w, eps=RMS_EPS):
            var = jnp.mean(jnp.square(h), axis=-1, keepdims=True)
            return h * jax.lax.rsqrt(var + eps) * w
        key = jax.random.key(seed)
        ks = jax.random.split(key, 5)
        x = jax.random.normal(ks[0], (B, N, D), dtype=jnp.float32)
        adjacency = jax.random.uniform(ks[1], (B, N, N), dtype=jnp.float32)
        epsilon = jnp.zeros((), dtype=jnp.float32)
        W1 = jax.random.normal(ks[2], (D, H), dtype=jnp.float32) * (1.0 / np.sqrt(D))
        b1 = jnp.zeros((H,), dtype=jnp.float32)
        rms_weight = jnp.ones((H,), dtype=jnp.float32)
        W2 = jax.random.normal(ks[3], (H, D), dtype=jnp.float32) * (1.0 / np.sqrt(H))
        b2 = jnp.zeros((D,), dtype=jnp.float32)
        return {'x': x, 'adjacency': adjacency, 'epsilon': epsilon, 'W1': W1, 'b1': b1, 'rms_weight': rms_weight, 'W2': W2, 'b2': b2}
    _L2_gnn_all = _L2_gnn_setup()
    _L2_gnn_in = {k: v for k, v in _L2_gnn_all.items() if k in ('epsilon', 'W1', 'b1', 'rms_weight', 'W2', 'b2', )}
    del _L2_gnn_all

    def _L3_gnn_setup():
        import jax, jax.numpy as jnp
        import numpy as np
        LN_EPS = 1e-05
        key = jax.random.key(seed)
        k1, k2, k3, k4 = jax.random.split(key, 4)
        B, N, F, O = (8, 2048, 256, 256)
        x = jax.random.normal(k1, (B, N, F), dtype=jnp.float32)
        adj = jax.random.uniform(k2, (B, N, N), dtype=jnp.float32)
        gamma = jnp.ones((F,), jnp.float32)
        beta = jnp.zeros((F,), jnp.float32)
        W_self = jax.random.normal(k3, (F, O), dtype=jnp.float32) * (1.0 / np.sqrt(F))
        W_neigh = jax.random.normal(k4, (F, O), dtype=jnp.float32) * (1.0 / np.sqrt(F))
        return {'x': x, 'adj': adj, 'gamma': gamma, 'beta': beta, 'W_self': W_self, 'W_neigh': W_neigh}
    _L3_gnn_all = _L3_gnn_setup()
    _L3_gnn_in = {k: v for k, v in _L3_gnn_all.items() if k in ('gamma', 'beta', 'W_self', 'W_neigh', )}
    del _L3_gnn_all

    return {
        "x": x,
        "adj": adj,
        "L0_gnn_Wq": _L0_gnn_in["Wq"],
        "L0_gnn_bq": _L0_gnn_in["bq"],
        "L0_gnn_Wk": _L0_gnn_in["Wk"],
        "L0_gnn_bk": _L0_gnn_in["bk"],
        "L0_gnn_Wv": _L0_gnn_in["Wv"],
        "L0_gnn_bv": _L0_gnn_in["bv"],
        "L0_gnn_Wo": _L0_gnn_in["Wo"],
        "L0_gnn_bo": _L0_gnn_in["bo"],
        "L1_gnn_eps": _L1_gnn_in["eps"],
        "L1_gnn_W1": _L1_gnn_in["W1"],
        "L1_gnn_b1": _L1_gnn_in["b1"],
        "L1_gnn_W2": _L1_gnn_in["W2"],
        "L1_gnn_b2": _L1_gnn_in["b2"],
        "L2_gnn_epsilon": _L2_gnn_in["epsilon"],
        "L2_gnn_W1": _L2_gnn_in["W1"],
        "L2_gnn_b1": _L2_gnn_in["b1"],
        "L2_gnn_rms_weight": _L2_gnn_in["rms_weight"],
        "L2_gnn_W2": _L2_gnn_in["W2"],
        "L2_gnn_b2": _L2_gnn_in["b2"],
        "L3_gnn_gamma": _L3_gnn_in["gamma"],
        "L3_gnn_beta": _L3_gnn_in["beta"],
        "L3_gnn_W_self": _L3_gnn_in["W_self"],
        "L3_gnn_W_neigh": _L3_gnn_in["W_neigh"],
    }

def reference(x, adj, L0_gnn_Wq, L0_gnn_bq, L0_gnn_Wk, L0_gnn_bk, L0_gnn_Wv, L0_gnn_bv, L0_gnn_Wo, L0_gnn_bo, L1_gnn_eps, L1_gnn_W1, L1_gnn_b1, L1_gnn_W2, L1_gnn_b2, L2_gnn_epsilon, L2_gnn_W1, L2_gnn_b1, L2_gnn_rms_weight, L2_gnn_W2, L2_gnn_b2, L3_gnn_gamma, L3_gnn_beta, L3_gnn_W_self, L3_gnn_W_neigh):
    import jax
    import jax.numpy as jnp
    def _L0_gnn_ref(x, adj, Wq, bq, Wk, bk, Wv, bv, Wo, bo):
        import jax, jax.numpy as jnp
        import numpy as np
        B, N = (1, 4096)
        D_IN, D_OUT, H = (256, 256, 8)
        HD = D_OUT // H
        NEG = -9000000000000000.0

        def _xavier(key, shape):
            lim = np.sqrt(6.0 / (shape[0] + shape[1])).astype(np.float32)
            return jax.random.uniform(key, shape, jnp.float32, -lim, lim)
        b, n, _ = x.shape

        def split_heads(t):
            return t.reshape(b, n, H, HD).transpose(0, 2, 1, 3)
        q = split_heads(x @ Wq + bq)
        k = split_heads(x @ Wk + bk)
        v = split_heads(x @ Wv + bv)
        scores = jnp.einsum('bhqd,bhkd->bhqk', q, k) / np.float32(np.sqrt(HD))
        scores = jnp.where(adj[:, None, :, :] > 0, scores, jnp.float32(NEG))
        attn = jax.nn.softmax(scores, axis=-1)
        out = jnp.einsum('bhqk,bhkd->bhqd', attn, v)
        out = out.transpose(0, 2, 1, 3).reshape(b, n, D_OUT)
        return out @ Wo + bo

    def _L1_gnn_ref(x, adj, eps, W1, b1, W2, b2):
        import jax, jax.numpy as jnp
        import numpy as np
        D_IN = 256
        D_HID = 512
        aggregated = jnp.einsum('bnm,bmd->bnd', adj, x)
        h = (1.0 + eps) * x + aggregated
        h = jax.nn.relu(h @ W1 + b1)
        return h @ W2 + b2

    def _L2_gnn_ref(x, adjacency, epsilon, W1, b1, rms_weight, W2, b2):
        import jax, jax.numpy as jnp
        import numpy as np
        B, N, D, H = (8, 2048, 256, 1024)
        RMS_EPS = 1e-06

        def _rmsnorm(h, w, eps=RMS_EPS):
            var = jnp.mean(jnp.square(h), axis=-1, keepdims=True)
            return h * jax.lax.rsqrt(var + eps) * w
        neighbor_sum = jnp.einsum('bnm,bmd->bnd', adjacency, x)
        agg = epsilon * x + neighbor_sum
        h = jnp.einsum('bnd,dh->bnh', agg, W1) + b1
        h = jax.nn.silu(_rmsnorm(h, rms_weight))
        out = jnp.einsum('bnh,hd->bnd', h, W2) + b2
        return out

    def _L3_gnn_ref(x, adj, gamma, beta, W_self, W_neigh):
        import jax, jax.numpy as jnp
        import numpy as np
        LN_EPS = 1e-05
        mu = jnp.mean(x, axis=-1, keepdims=True)
        var = jnp.mean(jnp.square(x - mu), axis=-1, keepdims=True)
        xn = (x - mu) * jax.lax.rsqrt(var + LN_EPS) * gamma + beta
        d_out = jnp.sum(adj, axis=1)
        d_in = jnp.sum(adj, axis=2)
        s_out = jnp.where(d_out != 0, jax.lax.rsqrt(d_out), 0.0)
        s_in = jnp.where(d_in != 0, jax.lax.rsqrt(d_in), 0.0)
        A_norm = s_out[:, :, None] * adj * s_in[:, None, :]
        eye = jnp.eye(adj.shape[1], dtype=adj.dtype)
        L = eye[None, :, :] - A_norm
        neighbor = jnp.einsum('bij,bjf->bif', L, xn)
        pre = xn @ W_self + neighbor @ W_neigh
        return jax.nn.softplus(pre)

    x = _layernorm(x + _L0_gnn_ref(x, adj, L0_gnn_Wq, L0_gnn_bq, L0_gnn_Wk, L0_gnn_bk, L0_gnn_Wv, L0_gnn_bv, L0_gnn_Wo, L0_gnn_bo), axis=-1)
    x = _layernorm(x + _L1_gnn_ref(x, adj, L1_gnn_eps, L1_gnn_W1, L1_gnn_b1, L1_gnn_W2, L1_gnn_b2), axis=-1)
    x = _layernorm(x + _L2_gnn_ref(x, adj, L2_gnn_epsilon, L2_gnn_W1, L2_gnn_b1, L2_gnn_rms_weight, L2_gnn_W2, L2_gnn_b2), axis=-1)
    x = _layernorm(x + _L3_gnn_ref(x, adj, L3_gnn_gamma, L3_gnn_beta, L3_gnn_W_self, L3_gnn_W_neigh), axis=-1)
    return x


_drawn_inputs = setup_inputs


def setup_inputs(seed=0):
    import zlib

    import numpy as np

    out = dict(_drawn_inputs(seed))
    spreads = {'L0_gnn_bq': (0.0, 0.1),
     'L0_gnn_bk': (0.0, 0.8),
     'L0_gnn_bv': (0.0, 0.1),
     'L0_gnn_bo': (0.0, 0.1),
     'L2_gnn_b1': (0.0, 0.8),
     'L2_gnn_rms_weight': (1.0, 0.2),
     'L2_gnn_b2': (0.0, 0.1),
     'L3_gnn_gamma': (1.0, 0.2),
     'L3_gnn_beta': (0.0, 0.1)}
    factors = {'L1_gnn_b1': 5.87}
    for name, (base, spread) in spreads.items():
        noise = np.random.default_rng([zlib.crc32(name.encode()), seed]).standard_normal(out[name].shape)
        drawn = base * np.exp(spread * noise) if base else spread * noise
        out[name] = jnp.asarray(drawn.astype(out[name].dtype))
    for name, factor in factors.items():
        out[name] = (out[name] * factor).astype(out[name].dtype)
    return out
```

```python
from contextlib import ExitStack

import concourse.bass as bass
from concourse import mybir

ALU = mybir.AluOpType
ACT = mybir.ActivationFunctionType
AX = mybir.AxisListType
F32 = mybir.dt.float32
F32R = mybir.dt.float32r

P = 128
N_GRAPHS, N, D = 32, 512, 256
NB = N // P
DC = D // P
HEADS, HD = 8, 32
GH = P // HD
H1, H2 = 512, 1024
HIDDEN = {1: H1 // P, 2: H2 // P}
PAIRS = N_GRAPHS // 2
NEG = -9000000000000000.0
SLOTS = (0, 1)
LN_EPS = 1e-5
RMS_EPS = 1e-6

SEGMENTS = [(s, g) for g in range(HEADS // GH) for s in SLOTS]
SEG_TILES = NB * GH
TILES = SEG_TILES * len(SEGMENTS)
LAG = 3
STREAM = TILES + 9
SCORE_BANKS, MASKED, PROBS = 3, 3, 4


def tile_of(i):
    s, g = SEGMENTS[i // SEG_TILES]
    return s, g, i % SEG_TILES // GH, i % GH


def qk_at(i):
    return {19: (0, 1, 0), 20: (0, 1, 1), 35: (1, 1, 0), 36: (1, 1, 1)}.get(i)


def segment_at(i, offset):
    q, r = divmod(i - offset, SEG_TILES)
    return q if r == 0 and 0 <= q < len(SEGMENTS) else None


class Signal:

    def __init__(self, sem, keys, by=1):
        self.sem, self.by, self.total = sem, by, len(keys) * by
        self.place = {k: (n + 1) * by for n, k in enumerate(keys)}
        self.keys, self.next = list(keys), 0

    def step(self, key):
        assert self.keys[self.next % len(self.keys)] == key, (key, self.keys[self.next % len(self.keys)])
        self.next += 1
        return self.sem, self.by

    def at(self, it, key, turns_back=0):
        return self.sem, it * self.total + (self.place[key] - turns_back * self.total)


def build(nc, x, adj, Wq, bq, Wk, bk, Wv, bv, Wo, bo, eps1, W1, b1, W2, b2,
          eps2, V1, c1, rms_w, V2, c2, gamma, beta, W_self, W_neigh, out):
    ctx = ExitStack()
    with ctx:
        def sb(name, shape, dt=F32):
            return ctx.enter_context(nc.sbuf_tensor(name, shape, dt))

        ident = sb("ident", [P, P])
        ones = sb("ones", [P, P])
        neg_half = sb("neg_half", [P, 8])
        diag = {1: sb("diag1", [P, P]), 2: sb("diag2", [P, P])}
        wq, wk, wv, wo = (sb(n, [P, DC, D]) for n in ("wq", "wk", "wv", "wo"))
        w_up = {1: sb("w1", [P, DC, H1]), 2: sb("v1", [P, DC, H2])}
        w_down = {1: sb("w2", [P, HIDDEN[1], D]), 2: sb("v2", [P, HIDDEN[2], D])}
        w_cat = sb("w_cat", [P, DC, 2 * D])
        gram = sb("gram", [P, DC, D])
        bqk = sb("bqk", [P, 2, DC])
        b_up = {1: sb("b1c", [P, HIDDEN[1]]), 2: sb("c1c", [P, HIDDEN[2]])}
        rms = sb("rms", [P, HIDDEN[2]])
        gb = sb("gb", [P, 2, DC])
        bv_rows = sb("bv_rows", [P, D])
        b_rows = {0: sb("bo_rows", [P, D]), 1: sb("b2_rows", [P, D]), 2: sb("c2_rows", [P, D])}
        eps_col = sb("eps_col", [P, 2])
        gram_c = sb("gram_c", [P, DC])
        sq_eps = sb("sq_eps", [P, 1])
        small = sb("small", [P, 16])

        def two(name, shape, dt=F32):
            return [sb(f"{name}{s}", shape, dt) for s in SLOTS]

        RES = two("res", [P, NB, D])
        XN = two("xn", [P, NB, D])
        ADJ = two("adj", [P, NB, N])
        ADJT = two("adjT", [P, NB, N], F32R)
        XT = two("xT", [P, DC, N])
        AG = two("ag", [P, DC, N])
        VN = two("vn", [P, NB, D])
        STK = two("stk", [P, 2, GH, N], F32R)
        STG = [sb(f"stg{w}", [P, 2, N], F32R) for w in range(2)]
        PT = sb("pT", [P, 2, GH, NB, 2 * P])
        SM = sb("masked", [P, MASKED, N])
        PR = sb("probs", [P, PROBS, N])
        REXP = sb("rexp", [P, N])
        RBS = sb("rbs", [P, N])
        NMAX = sb("nmax", [P, MASKED])
        RS = sb("rs", [P, 2, SEG_TILES])
        RR = sb("rr", [P, SEG_TILES])
        STATS = two("stats", [P, NB, 6])
        MV = two("mv", [P, NB, 2])
        VE = two("ve", [P, NB])
        RSTD = two("rstd", [P, NB])
        DEG = two("deg", [P, 2, NB])
        DNZ = two("dnz", [P, 2, NB])
        DSC = two("dsc", [P, 2, NB])
        DRS = two("drs", [P, 2, NB])
        NSO = two("nso", [P, NB])
        XH = [STK[s][:, 0, 0:2, :].rearrange("p a (b d) -> p (a b) d", d=D) for s in SLOTS]
        XL = [STK[s][:, 0, 2:4, :].rearrange("p a (b d) -> p (a b) d", d=D) for s in SLOTS]
        HB = [PT[:, 0, n, 0:2, :].rearrange("p a b -> p (a b)") for n in range(3)]
        ZB = [PT[:, 0, n, 2:4, :].rearrange("p a b -> p (a b)") for n in range(2)]
        RMSB = [REXP[:, :], RBS[:, :]]
        PA = [AG[s][:, :, :].rearrange("p c (b d) -> p (c b) d", d=D) for s in SLOTS]
        TMP = [XT[s][:, :, :].rearrange("p c (b d) -> p (c b) d", d=D) for s in SLOTS]
        GV = [VN[s][:, :, :].rearrange("p (c b) d -> p c (b d)", c=DC) for s in SLOTS]

        banks = [ctx.enter_context(nc.psum_tensor(f"bank{n}", [P, N], F32)) for n in range(8)]
        ACC = banks[4:8]
        OUT_T = banks[7]

        w_sem = ctx.enter_context(nc.semaphore("weights_loaded"))
        v_sem = ctx.enter_context(nc.semaphore("hidden_weights_loaded"))
        i_sem = ctx.enter_context(nc.semaphore("ident_ready"))
        t_sem = ctx.enter_context(nc.semaphore("v1T_in_psum"))
        u_sem = ctx.enter_context(nc.semaphore("v1T_copied"))
        g_sem = ctx.enter_context(nc.semaphore("gram_in_psum"))
        k_sem = ctx.enter_context(nc.semaphore("constants_done"))
        V1T = PT[:, 0, :, :, :].rearrange("p a b c -> p (a b c)").rearrange("p (k d) -> p k d", d=D)[:, 0:HIDDEN[2], :]

        def rows_to_all(v):
            return v.rearrange("(a n) -> a n", a=1)[0:1, :].to_broadcast([P, v.shape[0]])

        with nc.Block() as setup:
            @setup.sync
            def _(sp):
                sp.dma_start(w_up[2][:, :, :], V1.rearrange("(c p) n -> p c n", p=P)).then_inc(v_sem, 16)
                sp.dma_start(b_up[2][:, :], c1.rearrange("(c p) -> p c", p=P), allow_slow_non_contiguous=True).then_inc(v_sem, 16)
                n = 0
                for dst, src in ((wq, Wq), (wk, Wk), (wv, Wv), (wo, Wo), (w_up[1], W1)):
                    sp.dma_start(dst[:, :, :], src.rearrange("(c p) n -> p c n", p=P)).then_inc(w_sem, 16)
                for dst, src in ((w_down[1], W2), (w_down[2], V2)):
                    sp.dma_start(dst[:, :, :], src.rearrange("(c p) n -> p c n", p=P)).then_inc(w_sem, 16)
                for h, src in enumerate((W_self, W_neigh)):
                    sp.dma_start(w_cat[:, :, h * D:(h + 1) * D], src.rearrange("(c p) n -> p c n", p=P)).then_inc(w_sem, 16)
                for dst, src in ((bqk[:, 0, :], bq), (bqk[:, 1, :], bk), (b_up[1][:, :], b1), (rms[:, :], rms_w),
                                 (gb[:, 0, :], gamma), (gb[:, 1, :], beta)):
                    sp.dma_start(dst, src.rearrange("(c p) -> p c", p=P), allow_slow_non_contiguous=True).then_inc(w_sem, 16)
                for dst, src in ((bv_rows[:, :], bv), (b_rows[0][:, :], bo),
                                 (b_rows[1][:, :], b2), (b_rows[2][:, :], c2),
                                 (eps_col[:, 0:1], eps1), (eps_col[:, 1:2], eps2)):
                    sp.dma_start(dst, rows_to_all(src)).then_inc(w_sem, 16)
                sp.wait_ge(w_sem, 16 * 21)
                sp.wait_ge(v_sem, 32)

            @setup.gpsimd
            def _(pool):
                pool.memset(ident[:, :], 0.0).then_inc(i_sem, 1)
                pool.wait_ge(i_sem, 1)
                pool.affine_select(out=ident[:, :], in_=ident[:, :], compare_op=ALU.not_equal, fill=1.0,
                                   base=0, pattern=[[-1, P]], channel_multiplier=1).then_inc(i_sem, 1)
                pool.memset(ones[:, :], 1.0 / H2).then_inc(i_sem, 1)
                pool.memset(neg_half[:, :], -0.5).then_inc(i_sem, 1)
                pool.wait_ge(i_sem, 4)

            @setup.tensor
            def _(pe):
                pe.wait_ge(i_sem, 4)
                pe.wait_ge(v_sem, 32)
                for k in range(HIDDEN[2]):
                    for c in range(DC):
                        last = pe.transpose(banks[k // 2][:, (k % 2) * D + c * P:(k % 2) * D + (c + 1) * P],
                                            w_up[2][:, c, k * P:(k + 1) * P], ident[:, :])
                last.then_inc(t_sem, 1)
                pe.wait_ge(u_sem, 5)
                for c in range(DC):
                    for k in range(HIDDEN[2]):
                        pe.matmul(banks[4 + c][:, 0:D], V1T[:, k, c * P:(c + 1) * P], V1T[:, k, :],
                                  start=k == 0, stop=k == HIDDEN[2] - 1)
                    for k in range(HIDDEN[2]):
                        last = pe.matmul(banks[6 + c][:, 0:1], V1T[:, k, c * P:(c + 1) * P], b_up[2][:, k:k + 1],
                                         start=k == 0, stop=k == HIDDEN[2] - 1)
                last = pe.matmul(banks[0][:, 0:1], ones[:, :], small[:, 0:1], start=True, stop=True)
                last.then_inc(g_sem, 1)

            @setup.vector
            def _(dve):
                dve.wait_ge(t_sem, 1)
                for b in range(4):
                    dve.tensor_copy(V1T[:, 2 * b:2 * b + 2, :],
                                    banks[b][:, :].rearrange("p (k d) -> p k d", d=D)).then_inc(u_sem, 1)
                dve.tensor_tensor_reduce(small[:, 8:16], b_up[2][:, :], b_up[2][:, :], 1.0, 0.0, ALU.mult, ALU.add,
                                         small[:, 0:1]).then_inc(u_sem, 1)
                dve.wait_ge(w_sem, 16 * 21)
                dve.tensor_tensor(w_cat[:, :, 0:D], w_cat[:, :, 0:D], w_cat[:, :, D:2 * D], ALU.add).then_inc(k_sem, 1)
                dve.scalar_tensor_tensor(out=diag[1][:, :], in0=ident[:, :], scalar=eps_col[:, 0:1], in1=ident[:, :],
                                         op0=ALU.mult, op1=ALU.add).then_inc(k_sem, 1)
                dve.tensor_scalar(diag[2][:, :], ident[:, :], eps_col[:, 1:2], None, ALU.mult).then_inc(k_sem, 1)
                dve.wait_ge(g_sem, 1)
                for c in range(DC):
                    dve.tensor_copy(gram[:, c, :], banks[4 + c][:, 0:D]).then_inc(k_sem, 1)
                    dve.tensor_scalar(gram_c[:, c:c + 1], banks[6 + c][:, 0:1], 2.0, None, ALU.mult).then_inc(k_sem, 1)
                dve.tensor_scalar(sq_eps[:, :], banks[0][:, 0:1], RMS_EPS, None, ALU.add).then_inc(k_sem, 1)
                dve.wait_ge(k_sem, 8)

        signals = []

        def signal(name, keys, by=1):
            s = Signal(ctx.enter_context(nc.semaphore(name)), keys, by)
            signals.append(s)
            return s

        chunks = [(s, c) for s in SLOTS for c in range(DC)]
        blocks = [(s, b) for s in SLOTS for b in range(NB)]
        qks = [(s, 0, w) for s in SLOTS for w in range(2)] + [(s, 1, w) for s in SLOTS for w in range(2)]
        hids = [(L, s, k) for L in (1, 2) for s in SLOTS for k in range(HIDDEN[L])]
        layers = [(L, s) for L in range(5) for s in SLOTS]
        tiles = list(range(TILES))

        x_loaded = [signal(f"x_loaded{s}", ["x"], 16) for s in SLOTS]
        adj_loaded = [signal(f"adj_loaded{s}", ["adj"], 16) for s in SLOTS]
        stacked = [signal(f"stacked{w}", [(s, g, w, r, j) for s, g, ww in qks if ww == w for r in range(4) for j in range(GH)], 16)
                   for w in range(2)]
        stored = [signal(f"stored{s}", ["out"], 16) for s in SLOTS]

        pe_xT = signal("pe_xT", chunks)
        pe_adjT = signal("pe_adjT", blocks)
        pe_qk = signal("pe_qk", qks)
        pe_v = signal("pe_v", chunks)
        pe_scores = signal("pe_scores", tiles)
        pe_pT = signal("pe_pT", tiles)
        pe_av = signal("pe_av", range(TILES // 8))
        pe_rb = signal("pe_rb", range(4))
        pe_rows = signal("pe_rows", [(L, s) for L in (0, 3) for s in SLOTS])
        pe_agg = signal("pe_agg", [(L, s, c) for L in (1, 2) for s, c in chunks])
        pe_hid = signal("pe_hid", hids)
        pe_used = signal("pe_used", hids)
        pe_gram = signal("pe_gram", chunks)
        pe_ms = signal("pe_ms", SLOTS)
        pe_xnT = signal("pe_xnT", chunks)
        pe_p1 = signal("pe_p1", blocks)

        act_adjT = signal("act_adjT", blocks)
        act_hi = signal("act_hi", qks)
        act_exp = signal("act_exp", tiles)
        act_pT = signal("act_pT", [i for i in tiles if i % 2])
        act_rb = signal("act_rb", range(4))
        act_xh = signal("act_xh", [(L, s) for L in range(2) for s in SLOTS])
        act_agg = signal("act_agg", [(L, s) for L in (1, 2) for s in SLOTS])
        act_hid = signal("act_hid", hids)
        act_rms = signal("act_rms", [(s, n) for n in range(2) for s in SLOTS])
        act_p1 = signal("act_p1", blocks)
        act_soft = signal("act_soft", [(s, n) for s in SLOTS for n in range(3)])

        dve_xT = signal("dve_xT", chunks)
        dve_din = signal("dve_din", SLOTS)
        dve_lo = signal("dve_lo", qks)
        dve_mask = signal("dve_mask", SLOTS)
        dve_v = signal("dve_v", chunks)
        dve_max = signal("dve_max", tiles)
        dve_pT = signal("dve_pT", [i for i in tiles if i % 2 == 0])
        dve_recip = signal("dve_recip", [(q, n) for q in range(4) for n in range(2)])
        dve_attn = signal("dve_attn", range(4))
        dve_add = signal("dve_add", [(L, s, b) for L in range(3) for s, b in blocks])
        dve_stat = signal("dve_stat", [(L, s, b) for L in (0, 1) for s, b in blocks]
                          + [(L, s, b) for s in SLOTS for L in (2, 3) for b in range(NB)] + [(4, s, b) for s, b in blocks])
        dve_aggr = signal("dve_aggr", dve_stat.keys)
        dve_norm = signal("dve_norm", dve_stat.keys)
        dve_xl = signal("dve_xl", [(L, s) for L in range(2) for s in SLOTS])
        dve_agg = signal("dve_agg", [(L, s) for L in (1, 2) for s in SLOTS])
        dve_gram = signal("dve_gram", chunks)
        dve_z = signal("dve_z", [(s, k) for s in SLOTS for k in range(HIDDEN[2])])
        dve_xnT = signal("dve_xnT", chunks)
        dve_yl = signal("dve_yl", blocks)
        dve_pre = signal("dve_pre", blocks)
        dve_soft = signal("dve_soft", [(s, n) for s in SLOTS for n in range(2)])

        ln_order = [(0, 0), (0, 1), (1, 0), (1, 1), (2, 0), (3, 0), (2, 1), (3, 1), (4, 0), (4, 1)]
        pool_res = signal("pool_res", [(L, s) for L in range(3) for s in SLOTS])
        pool_var = signal("pool_var", ln_order)
        pool_rstd = signal("pool_rstd", ln_order)
        pool_deg = signal("pool_deg", [(s, n) for s in SLOTS for n in range(6)])

        work = []
        work += [(("xT", s, c), dve_xT, (s, c)) for s, c in chunks]
        for s in SLOTS:
            work += [(("adjT", s, b), act_adjT, (s, b)) for b in range(NB)]
            work += [(("qk", s, 0, w), dve_lo, (s, 0, w)) for w in range(2)]
            work += [(("v", s, c), dve_v, (s, c)) for c in range(2)]
        for i in range(STREAM):
            t = i - LAG
            if 0 <= t < TILES:
                work.append((("pT", t), act_pT if t % 2 else dve_pT, t))
            if qk_at(i):
                work.append((("qk", *qk_at(i)), dve_lo, qk_at(i)))
            if (q := segment_at(i, 21)) is not None:
                work.append((("rb", q), act_rb, q))
        for L in (1, 2):
            work += [(("agg", L, s, c), act_agg if c == 0 else dve_agg, (L, s)) for s, c in chunks]
            if L == 2:
                work += [(("gram", s, c), dve_gram, (s, c)) for s, c in chunks]
                work += [(("ms", s), act_rms, (s, 0)) for s in SLOTS]
            work += [(("hid", LL, s, k), act_hid if L == 1 else dve_z, (LL, s, k) if L == 1 else (s, k))
                     for LL, s, k in hids if LL == L]
        for s in SLOTS:
            work += [(("xnT", s, c), dve_xnT, (s, c)) for c in range(DC)]
            work += [(("p1", s, b), dve_yl, (s, b)) for b in range(NB)]
        while len(work) % 4:
            work.append((None, None, None))
        place = {w[0]: n for n, w in enumerate(work)}

        def work_bank(key):
            return banks[place[key] % 4]

        def bank_read(it, key):
            n, back = place[key] - 4, 0
            while n < 0 or work[n][0] is None:
                if n < 0:
                    n, back = n + len(work), 1
                else:
                    n -= 4
            return work[n][1].at(it, work[n][2], back)

        x_v = x.rearrange("g (t p) d -> g p t d", p=P)
        adj_v = adj.rearrange("g (t p) m -> g p t m", p=P)
        out_v = out.rearrange("g (t p) d -> g p t d", p=P)

        with nc.Block() as block:
            @block.sync
            def _(sp):
                for s in signals:
                    if s not in x_loaded and s not in adj_loaded:
                        sp.sem_inc(s.sem, s.total)
                for s in SLOTS:
                    sp.dma_start(RES[s][:, :, :], x_v[s]).then_inc(x_loaded[s].sem, 16)
                for s in SLOTS:
                    sp.dma_start(ADJ[s][:, :, :], adj_v[s]).then_inc(adj_loaded[s].sem, 16)
                with sp.Fori(1, PAIRS + 1) as it:
                    pair = sp.snap(it & (PAIRS - 1))
                    following = [sp.snap(pair * 2 + s) for s in SLOTS]
                    present = [sp.snap(it * 2 + (s - 2)) for s in SLOTS]
                    for s in SLOTS:
                        sp.compute_val(following[s])
                        sp.compute_val(present[s])
                    for s, g, w in qks:
                        if g:
                            free = pe_scores.at(it, SEG_TILES * SEGMENTS.index((s, 0)) + SEG_TILES - 1)
                        else:
                            free = pe_rows.at(it, (3, s), 1)
                        sp.compute_val(free[1])
                        sp.compute_val(dve_lo.at(it, (s, g, w))[1])
                        sp.wait_ge(*free)
                        sp.wait_ge(*dve_lo.at(it, (s, g, w)))
                        for r in range(4):
                            part = r % 2 if w == 0 else r // 2
                            for j in range(GH):
                                sp.dma_start(STK[s][r * HD:(r + 1) * HD, w, j, :].bitcast(F32),
                                                             STG[w][j * HD:(j + 1) * HD, part, :].bitcast(F32)).then_inc(*stacked[w].step((s, g, w, r, j)))
                    for s in SLOTS:
                        sp.wait_ge(*dve_max.at(it, SEG_TILES * SEGMENTS.index((s, 1)) + SEG_TILES - 1))
                        sp.dma_start(ADJ[s][:, :, :], adj_v[following[s]]).then_inc(*adj_loaded[s].step("adj"))
                    for s in SLOTS:
                        sp.wait_ge(*dve_norm.at(it, (2, s, NB - 1)))
                        sp.dma_start(RES[s][:, :, :], x_v[following[s]]).then_inc(*x_loaded[s].step("x"))
                    for s in SLOTS:
                        sp.wait_ge(*dve_norm.at(it, (4, s, NB - 1)))
                        sp.dma_start(out_v[present[s]], VN[s][:, :, :]).then_inc(*stored[s].step("out"))
                for s in SLOTS:
                    sp.wait_ge(stored[s].sem, 16 * (PAIRS + 1))
                    sp.wait_ge(x_loaded[s].sem, 16 * (PAIRS + 1))
                    sp.wait_ge(adj_loaded[s].sem, 16 * (PAIRS + 1))

            @block.tensor
            def _(pe):
                def project_qk(it, s, g, w):
                    bank = work_bank(("qk", s, g, w))
                    pe.wait_ge(*bank_read(it, ("qk", s, g, w)))
                    for c in range(DC):
                        last = pe.matmul(bank[:, :], (wq, wk)[w][:, c, g * P:(g + 1) * P], XT[s][:, c, :],
                                         start=c == 0, stop=c == DC - 1)
                    last.then_inc(*pe_qk.step((s, g, w)))

                with pe.Fori(1, PAIRS + 1) as it:
                    for s in SLOTS:
                        pe.wait_ge(*x_loaded[s].at(it, "x", 1))
                        for c in range(DC):
                            bank = work_bank(("xT", s, c))
                            pe.wait_ge(*bank_read(it, ("xT", s, c)))
                            for b in range(NB):
                                last = pe.transpose(bank[:, b * P:(b + 1) * P], RES[s][:, b, c * P:(c + 1) * P], ident[:, :])
                            last.then_inc(*pe_xT.step((s, c)))
                    for s in SLOTS:
                        pe.wait_ge(*adj_loaded[s].at(it, "adj", 1))
                        for m in range(NB):
                            bank = work_bank(("adjT", s, m))
                            pe.wait_ge(*bank_read(it, ("adjT", s, m)))
                            for b in range(NB):
                                last = pe.transpose(bank[:, b * P:(b + 1) * P], ADJ[s][:, b, m * P:(m + 1) * P], ident[:, :])
                            last.then_inc(*pe_adjT.step((s, m)))
                        pe.wait_ge(*dve_xT.at(it, (s, DC - 1)))
                        for w in range(2):
                            project_qk(it, s, 0, w)
                        for half in range(2):
                            bank = work_bank(("v", s, half))
                            pe.wait_ge(*bank_read(it, ("v", s, half)))
                            for b in range(2):
                                for c in range(DC):
                                    nb = 2 * half + b
                                    last = pe.matmul(bank[:, b * D:(b + 1) * D], XT[s][:, c, nb * P:(nb + 1) * P],
                                                     wv[:, c, :], start=c == 0, stop=c == DC - 1)
                            last.then_inc(*pe_v.step((s, half)))

                    for i in range(STREAM):
                        if i < TILES:
                            s, g, b, j = tile_of(i)
                            if i % SEG_TILES == 0:
                                for w in range(2):
                                    pe.wait_ge(*stacked[w].at(it, (s, g, w, 3, GH - 1)))
                            if i < SCORE_BANKS:
                                pe.wait_ge(*dve_pre.at(it, (1, NB - 1), 1))
                            else:
                                pe.wait_ge(*dve_max.at(it, i - SCORE_BANKS))
                            pe.matmul(banks[4 + i % SCORE_BANKS][:, :], STK[s][:, 0, j, b * P:(b + 1) * P],
                                                     STK[s][:, 1, j, :], start=True, stop=True).then_inc(*pe_scores.step(i))
                        t = i - LAG
                        if 0 <= t < TILES:
                            bank = work_bank(("pT", t))
                            pe.wait_ge(*bank_read(it, ("pT", t)))
                            pe.wait_ge(*act_exp.at(it, t))
                            for k in range(NB):
                                last = pe.transpose(bank[:, k * P:(k + 1) * P], PR[:, t % PROBS, k * P:(k + 1) * P], ident[:, :])
                            last.then_inc(*pe_pT.step(t))
                        if qk_at(i):
                            project_qk(it, *qk_at(i))
                        p, k = divmod(i - 12, 8)
                        if k < NB and 0 <= p < TILES // 8:
                            s, g, b, _ = tile_of(8 * p)
                            if k == 0:
                                pe.wait_ge(*act_pT.at(it, 8 * p + 7))
                                pe.wait_ge(*dve_pT.at(it, 8 * p + 6))
                                pe.wait_ge(*dve_v.at(it, (s, DC - 1)))
                                if p == 0:
                                    pe.wait_ge(*dve_pre.at(it, (1, NB - 1), 1))
                                elif p % 2 == 0:
                                    pe.wait_ge(*dve_attn.at(it, p // 2 - 1))
                            for j in range(GH):
                                h = g * GH + j
                                last = pe.matmul(OUT_T[j * HD:(j + 1) * HD, b * P:(b + 2) * P],
                                                 VN[s][:, k, h * HD:(h + 1) * HD], PT[:, p % 2, j, k, :],
                                                 start=k == 0, stop=k == NB - 1)
                            if k == NB - 1:
                                last.then_inc(*pe_av.step(p))
                        if (q := segment_at(i, 21)) is not None:
                            bank = work_bank(("rb", q))
                            pe.wait_ge(*bank_read(it, ("rb", q)))
                            pe.wait_ge(*dve_recip.at(it, (q, 1)))
                            for b in range(NB):
                                last = pe.transpose(bank[:, b * P:(b + 1) * P], REXP[:, b * P:(b + 1) * P], ident[:, :])
                            last.then_inc(*pe_rb.step(q))

                    for s in SLOTS:
                        pe.wait_ge(*dve_attn.at(it, 2 + s))
                        if s == 0:
                            pe.wait_ge(*dve_max.at(it, TILES - 1))
                            pe.wait_ge(*dve_attn.at(it, 3))
                        else:
                            pe.wait_ge(*dve_add.at(it, (0, 0, NB - 1)))
                        for b in range(NB):
                            for c in range(DC):
                                last = pe.matmul(ACC[b][:, 0:D], AG[s][:, c, b * P:(b + 1) * P], wo[:, c, :],
                                                 start=c == 0, stop=c == DC - 1)
                        last.then_inc(*pe_rows.step((0, s)))

                    for L in (1, 2):
                        for s in SLOTS:
                            pe.wait_ge(*act_adjT.at(it, (s, NB - 1)))
                            pe.wait_ge(*dve_xl.at(it, (L - 1, s)))
                            for c in range(DC):
                                bank = work_bank(("agg", L, s, c))
                                pe.wait_ge(*bank_read(it, ("agg", L, s, c)))
                                for m in range(NB):
                                    for n, part in enumerate((XH, XL)):
                                        pe.matmul(bank[:, :], part[s][:, m, c * P:(c + 1) * P], ADJT[s][:, m, :],
                                                  start=m == 0 and n == 0, stop=False)
                                for m in range(NB):
                                    last = pe.matmul(bank[:, m * P:(m + 1) * P], XN[s][:, m, c * P:(c + 1) * P], diag[L][:, :],
                                                     start=False, stop=m == NB - 1)
                                last.then_inc(*pe_agg.step((L, s, c)))
                        if L == 2:
                            for s in SLOTS:
                                pe.wait_ge(*act_agg.at(it, (L, s)))
                                pe.wait_ge(*dve_agg.at(it, (L, s)))
                                for c in range(DC):
                                    bank = work_bank(("gram", s, c))
                                    pe.wait_ge(*bank_read(it, ("gram", s, c)))
                                    for e in range(DC):
                                        last = pe.matmul(bank[:, :], gram[:, e, c * P:(c + 1) * P], AG[s][:, e, :],
                                                         start=e == 0, stop=e == DC - 1)
                                    last.then_inc(*pe_gram.step((s, c)))
                            for s in SLOTS:
                                bank = work_bank(("ms", s))
                                pe.wait_ge(*bank_read(it, ("ms", s)))
                                for c in range(DC):
                                    pe.wait_ge(*dve_gram.at(it, (s, c)))
                                    last = pe.matmul(bank[:, :], ones[:, :], GV[s][:, c, :], start=c == 0, stop=c == DC - 1)
                                last.then_inc(*pe_ms.step(s))
                        for s in SLOTS:
                            pe.wait_ge(*act_agg.at(it, (L, s)))
                            pe.wait_ge(*dve_agg.at(it, (L, s)))
                            for k in range(HIDDEN[L] + 2):
                                if k < HIDDEN[L]:
                                    bank = work_bank(("hid", L, s, k))
                                    pe.wait_ge(*bank_read(it, ("hid", L, s, k)))
                                    for c in range(DC):
                                        last = pe.matmul(bank[:, :], w_up[L][:, c, k * P:(k + 1) * P], AG[s][:, c, :],
                                                         start=c == 0, stop=c == DC - 1)
                                    last.then_inc(*pe_hid.step((L, s, k)))
                                if k >= 2:
                                    h = k - 2
                                    pe.wait_ge(*act_hid.at(it, (L, s, h)))
                                    if h == 0:
                                        pe.wait_ge(*dve_add.at(it, (L, 0, NB - 1) if s else (L - 1, 1, NB - 1)))
                                    slot = hids.index((L, s, h)) % 3
                                    for b in range(NB):
                                        last = pe.matmul(ACC[b][:, 0:D], HB[slot][:, b * P:(b + 1) * P], w_down[L][:, h, :],
                                                         start=h == 0, stop=h == HIDDEN[L] - 1)
                                    last.then_inc(*pe_used.step((L, s, h)))

                    for s in SLOTS:
                        pe.wait_ge(*dve_norm.at(it, (3, s, NB - 1)))
                        for c in range(DC):
                            bank = work_bank(("xnT", s, c))
                            pe.wait_ge(*bank_read(it, ("xnT", s, c)))
                            for b in range(NB):
                                last = pe.transpose(bank[:, b * P:(b + 1) * P], VN[s][:, b, c * P:(c + 1) * P], ident[:, :])
                            last.then_inc(*pe_xnT.step((s, c)))
                        for b in range(NB):
                            bank = work_bank(("p1", s, b))
                            pe.wait_ge(*bank_read(it, ("p1", s, b)))
                            pe.wait_ge(*dve_xnT.at(it, (s, DC - 1)))
                            for c in range(DC):
                                last = pe.matmul(bank[:, :], XT[s][:, c, b * P:(b + 1) * P], w_cat[:, c, :],
                                                 start=c == 0, stop=c == DC - 1)
                            last.then_inc(*pe_p1.step((s, b)))
                        if s == 0:
                            pe.wait_ge(*dve_add.at(it, (2, 1, NB - 1)))
                        else:
                            pe.wait_ge(*dve_pre.at(it, (0, NB - 1)))
                        pe.wait_ge(*dve_yl.at(it, (s, NB - 1)))
                        for b in range(NB):
                            for m in range(NB):
                                for n, part in enumerate((XH, XL)):
                                    last = pe.matmul(ACC[b][:, 0:D], ADJT[s][:, m, b * P:(b + 1) * P], part[s][:, m, :],
                                                     start=m == 0 and n == 0, stop=m == NB - 1 and n == 1)
                        last.then_inc(*pe_rows.step((3, s)))

            @block.scalar
            def _(act):
                def hi_part(it, s, g, w):
                    act.wait_ge(*pe_qk.at(it, (s, g, w)))
                    n = [q for q in qks if q[2] == w].index((s, g, w))
                    before = [q for q in qks if q[2] == w][n - 1]
                    act.wait_ge(*stacked[w].at(it, (*before, 3, GH - 1), 1 if n == 0 else 0))
                    act.activation(STG[w][:, 0, :], work_bank(("qk", s, g, w))[:, :], ACT.Identity,
                                               bias=bqk[:, w, g:g + 1]).then_inc(*act_hi.step((s, g, w)))

                def x_hi(it, L, s):
                    act.wait_ge(*dve_norm.at(it, (L, s, NB - 1)))
                    act.activation(XH[s], XN[s][:, :, :], ACT.Copy).then_inc(*act_xh.step((L, s)))

                def sums(it, L, s):
                    act.wait_ge(*pe_agg.at(it, (L, s, 0)))
                    act.activation(AG[s][:, 0, :], work_bank(("agg", L, s, 0))[:, :], ACT.Copy).then_inc(*act_agg.step((L, s)))

                def hidden_free(it, L, s, k):
                    n = hids.index((L, s, k)) - 3
                    if n >= 0:
                        act.wait_ge(*pe_used.at(it, hids[n]))

                with act.Fori(1, PAIRS + 1) as it:
                    for s in SLOTS:
                        for m in range(NB):
                            if m == 0:
                                act.wait_ge(*pe_rows.at(it, (3, s), 1))
                                act.wait_ge(*pool_deg.at(it, (s, 5), 1))
                            act.wait_ge(*pe_adjT.at(it, (s, m)))
                            act.activation(ADJT[s][:, m, :], work_bank(("adjT", s, m))[:, :], ACT.Copy,
                                                         accum_out=DEG[s][:, 0, m:m + 1]).then_inc(*act_adjT.step((s, m)))
                        for w in range(2):
                            hi_part(it, s, 0, w)

                    for i in range(STREAM):
                        if i < TILES:
                            act.wait_ge(*dve_max.at(it, i))
                            if i >= PROBS:
                                act.wait_ge(*pe_pT.at(it, i - PROBS))
                            act.activation(PR[:, i % PROBS, :], SM[:, i % MASKED, :], ACT.Exp, scale=-1.0,
                                                        bias=NMAX[:, i % MASKED:i % MASKED + 1],
                                                        accum_out=RS[:, i // SEG_TILES % 2, i % SEG_TILES:i % SEG_TILES + 1]).then_inc(*act_exp.step(i))
                        t = i - LAG
                        if 0 <= t < TILES and t % 2:
                            act.wait_ge(*pe_pT.at(it, t))
                            _, _, b, j = tile_of(t)
                            act.activation(PT[:, t // 8 % 2, j, :, b % 2 * P:(b % 2 + 1) * P],
                                                       work_bank(("pT", t))[:, :].rearrange("p (k q) -> p k q", q=P), ACT.Copy).then_inc(*act_pT.step(t))
                        if qk_at(i):
                            hi_part(it, *qk_at(i))
                        if (q := segment_at(i, 22)) is not None:
                            act.wait_ge(*pe_rb.at(it, q))
                            if q:
                                act.wait_ge(*dve_attn.at(it, q - 1))
                            act.activation(RBS[:, :], work_bank(("rb", q))[:, :], ACT.Copy).then_inc(*act_rb.step(q))

                    for s in SLOTS:
                        x_hi(it, 0, s)
                    for s in SLOTS:
                        sums(it, 1, s)
                    for s in SLOTS:
                        for k in range(HIDDEN[1]):
                            act.wait_ge(*pe_hid.at(it, (1, s, k)))
                            hidden_free(it, 1, s, k)
                            act.activation(HB[hids.index((1, s, k)) % 3], work_bank(("hid", 1, s, k))[:, :],
                                                        ACT.Relu, bias=b_up[1][:, k:k + 1]).then_inc(*act_hid.step((1, s, k)))
                    for s in SLOTS:
                        x_hi(it, 1, s)
                        sums(it, 2, s)
                    for s in SLOTS:
                        act.wait_ge(*pe_ms.at(it, s))
                        act.activation(RMSB[s], work_bank(("ms", s))[:, :], ACT.Ln, bias=sq_eps[:, :]).then_inc(*act_rms.step((s, 0)))
                    for s in SLOTS:
                        act.wait_ge(*act_rms.at(it, (s, 0)))
                        act.activation(RMSB[s], RMSB[s], ACT.Exp, scale=-0.5).then_inc(*act_rms.step((s, 1)))
                    for s in SLOTS:
                        for k in range(HIDDEN[2]):
                            act.wait_ge(*dve_z.at(it, (s, k)))
                            hidden_free(it, 2, s, k)
                            act.activation(HB[hids.index((2, s, k)) % 3], ZB[k % 2], ACT.Silu,
                                                        scale=rms[:, k:k + 1]).then_inc(*act_hid.step((2, s, k)))
                    for s in SLOTS:
                        for b in range(NB):
                            act.wait_ge(*pe_p1.at(it, (s, b)))
                            if b == 0:
                                act.wait_ge(*pool_deg.at(it, (s, 5)))
                            bank = work_bank(("p1", s, b))
                            act.activation(XH[s][:, b, :], bank[:, D:2 * D], ACT.Copy, scale=DRS[s][:, 1, b:b + 1])
                            act.activation(PA[s][:, b, :], bank[:, 0:D], ACT.Copy).then_inc(*act_p1.step((s, b)))
                        act.wait_ge(*dve_pre.at(it, (s, NB - 1)))
                        act.activation(TMP[s], PA[s], ACT.Abs).then_inc(*act_soft.step((s, 0)))
                        act.wait_ge(*act_soft.at(it, (s, 0)))
                        act.activation(TMP[s], TMP[s], ACT.Exp, scale=-1.0).then_inc(*act_soft.step((s, 1)))
                        act.wait_ge(*act_soft.at(it, (s, 1)))
                        act.activation(TMP[s], TMP[s], ACT.Ln, bias=1.0).then_inc(*act_soft.step((s, 2)))

            @block.vector
            def _(dve):
                def lo_part(it, s, g, w):
                    dve.wait_ge(*act_hi.at(it, (s, g, w)))
                    dve.scalar_tensor_tensor(out=STG[w][:, 1, :], in0=work_bank(("qk", s, g, w))[:, :],
                                                         scalar=bqk[:, w, g:g + 1], in1=STG[w][:, 0, :],
                                                         op0=ALU.add, op1=ALU.subtract).then_inc(*dve_lo.step((s, g, w)))

                def norm_source(L, s):
                    return RES[s] if L < 3 else XN[s] if L == 3 else PA[s]

                def statistics(it, L, s):
                    src = norm_source(L, s)
                    if L < 3:
                        if L == 0:
                            dve.wait_ge(*pe_rows.at(it, (0, s)))
                        else:
                            dve.wait_ge(*pe_used.at(it, (L, s, HIDDEN[L] - 1)))
                        dve.wait_ge(*pool_res.at(it, (L, s)))
                        for b in range(NB):
                            dve.tensor_tensor(RES[s][:, b, :], ACC[b][:, 0:D], RES[s][:, b, :], ALU.add).then_inc(*dve_add.step((L, s, b)))
                    for b in range(NB):
                        if L < 3:
                            dve.wait_ge(*dve_add.at(it, (L, s, b)))
                        elif L == 3:
                            dve.wait_ge(*dve_norm.at(it, (2, s, b)))
                        elif b == 0:
                            dve.wait_ge(*dve_soft.at(it, (s, 1)))
                        dve.bn_stats(STATS[s][:, b, :], src[:, b, :]).then_inc(*dve_stat.step((L, s, b)))
                    for b in range(NB):
                        dve.compute_val(dve_stat.at(it, (L, s, b))[1])
                        dve.wait_ge(k_sem, 8)
                        dve.wait_ge(*dve_stat.at(it, (L, s, b)))
                        dve.bn_aggr(MV[s][:, b, :], STATS[s][:, b, :]).then_inc(*dve_aggr.step((L, s, b)))

                def normalise(it, L, s):
                    src, dst = norm_source(L, s), XN[s] if L < 3 else VN[s]
                    dve.wait_ge(*pool_rstd.at(it, (L, s)))
                    for b in range(NB):
                        dve.tensor_scalar(dst[:, b, :], src[:, b, :], MV[s][:, b, 0:1], RSTD[s][:, b:b + 1],
                                                        ALU.subtract, ALU.mult).then_inc(*dve_norm.step((L, s, b)))

                def x_lo(it, L, s):
                    dve.wait_ge(*act_xh.at(it, (L, s)))
                    dve.tensor_tensor(XL[s], XN[s][:, :, :], XH[s], ALU.subtract).then_inc(*dve_xl.step((L, s)))

                def sums(it, L, s):
                    dve.wait_ge(*pe_agg.at(it, (L, s, 1)))
                    dve.tensor_copy(AG[s][:, 1, :], work_bank(("agg", L, s, 1))[:, :]).then_inc(*dve_agg.step((L, s)))

                def scaled_hidden(it, s, k):
                    if k == 0:
                        dve.wait_ge(*act_rms.at(it, (s, 1)))
                    dve.wait_ge(*pe_hid.at(it, (2, s, k)))
                    n = hids.index((2, s, k)) - 2
                    if hids[n][0] == 2:
                        dve.wait_ge(*act_hid.at(it, hids[n]))
                    dve.scalar_tensor_tensor(out=ZB[k % 2], in0=work_bank(("hid", 2, s, k))[:, :],
                                                        scalar=b_up[2][:, k:k + 1], in1=RMSB[s],
                                                        op0=ALU.add, op1=ALU.mult).then_inc(*dve_z.step((s, k)))

                def xn_transposed(it, s):
                    for c in range(DC):
                        dve.wait_ge(*pe_xnT.at(it, (s, c)))
                        dve.tensor_scalar(XT[s][:, c, :], work_bank(("xnT", s, c))[:, :], gb[:, 0, c:c + 1],
                                                       gb[:, 1, c:c + 1], ALU.mult, ALU.add).then_inc(*dve_xnT.step((s, c)))

                def y_lo(it, s, b):
                    dve.wait_ge(*act_p1.at(it, (s, b)))
                    dve.scalar_tensor_tensor(out=XL[s][:, b, :], in0=work_bank(("p1", s, b))[:, D:2 * D],
                                                         scalar=DRS[s][:, 1, b:b + 1], in1=XH[s][:, b, :],
                                                         op0=ALU.mult, op1=ALU.subtract).then_inc(*dve_yl.step((s, b)))

                def pre_activation(it, s):
                    dve.wait_ge(*pe_rows.at(it, (3, s)))
                    for b in range(NB):
                        dve.scalar_tensor_tensor(out=PA[s][:, b, :], in0=ACC[b][:, 0:D], scalar=NSO[s][:, b:b + 1],
                                                              in1=PA[s][:, b, :], op0=ALU.mult, op1=ALU.add).then_inc(*dve_pre.step((s, b)))

                def residual(it, s):
                    dve.wait_ge(*act_soft.at(it, (s, 2)))
                    dve.scalar_tensor_tensor(out=PA[s], in0=PA[s], scalar=0.0, in1=TMP[s],
                                                           op0=ALU.max, op1=ALU.add).then_inc(*dve_soft.step((s, 0)))
                    dve.wait_ge(*dve_soft.at(it, (s, 0)))
                    dve.tensor_tensor(PA[s], PA[s], XN[s][:, :, :], ALU.add).then_inc(*dve_soft.step((s, 1)))

                with dve.Fori(1, PAIRS + 1) as it:
                    for s, c in chunks:
                        dve.wait_ge(*pe_xT.at(it, (s, c)))
                        dve.tensor_copy(XT[s][:, c, :], work_bank(("xT", s, c))[:, :]).then_inc(*dve_xT.step((s, c)))
                    for s in SLOTS:
                        dve.wait_ge(*adj_loaded[s].at(it, "adj", 1))
                        dve.wait_ge(*pool_deg.at(it, (s, 5), 1))
                        dve.tensor_reduce(DEG[s][:, 1, :], ADJ[s][:, :, :], AX.X, ALU.add).then_inc(*dve_din.step(s))
                        for w in range(2):
                            lo_part(it, s, 0, w)
                        dve.wait_ge(*pe_adjT.at(it, (s, NB - 1)))
                        dve.wait_ge(*dve_din.at(it, s))
                        dve.tensor_scalar(ADJ[s][:, :, :], ADJ[s][:, :, :], 0.0, NEG, ALU.is_le, ALU.mult).then_inc(*dve_mask.step(s))
                        for half in range(2):
                            dve.wait_ge(*pe_v.at(it, (s, half)))
                            if half == 0:
                                dve.wait_ge(*stored[s].at(it, "out", 1))
                            dve.tensor_tensor(VN[s][:, 2 * half:2 * half + 2, :],
                                                         work_bank(("v", s, half))[:, :].rearrange("p (b d) -> p b d", d=D),
                                                         bv_rows[:, :].unsqueeze(1).to_broadcast([P, 2, D]), ALU.add).then_inc(*dve_v.step((s, half)))

                    for i in range(STREAM):
                        if i < TILES:
                            s, g, b, j = tile_of(i)
                            if i % SEG_TILES == 0:
                                dve.wait_ge(*dve_mask.at(it, s))
                            if i >= MASKED:
                                dve.wait_ge(*act_exp.at(it, i - MASKED))
                            dve.compute_val(pe_scores.at(it, i)[1])
                            dve.wait_ge(k_sem, 8)
                            dve.wait_ge(*pe_scores.at(it, i))
                            dve.tensor_tensor_reduce(
                                SM[:, i % MASKED, :], banks[4 + i % SCORE_BANKS][:, :], ADJ[s][:, b, :], -float(HD) ** -0.5,
                                3.0e38, ALU.add, ALU.min, NMAX[:, i % MASKED:i % MASKED + 1]).then_inc(*dve_max.step(i))
                        t = i - LAG
                        if 0 <= t < TILES and t % 2 == 0:
                            dve.wait_ge(*pe_pT.at(it, t))
                            _, _, b, j = tile_of(t)
                            dve.tensor_copy(PT[:, t // 8 % 2, j, :, b % 2 * P:(b % 2 + 1) * P],
                                                        work_bank(("pT", t))[:, :].rearrange("p (k q) -> p k q", q=P)).then_inc(*dve_pT.step(t))
                        if qk_at(i):
                            lo_part(it, *qk_at(i))
                        if (q := segment_at(i, 18)) is not None:
                            dve.wait_ge(*act_exp.at(it, SEG_TILES * q + SEG_TILES - 1))
                            dve.reciprocal(RR[:, :], RS[:, q % 2, :]).then_inc(*dve_recip.step((q, 0)))
                            dve.wait_ge(*dve_recip.at(it, (q, 0)))
                            if q:
                                dve.wait_ge(*pe_rb.at(it, q - 1))
                            dve.tensor_copy(REXP[:, :].rearrange("p (t d) -> p t d", d=HD),
                                                           RR[:, :].unsqueeze(2).to_broadcast([P, SEG_TILES, HD])).then_inc(*dve_recip.step((q, 1)))
                        if (q := segment_at(i, 24)) is not None:
                            s, g = SEGMENTS[q]
                            dve.wait_ge(*act_rb.at(it, q))
                            dve.wait_ge(*pe_av.at(it, 2 * q + 1))
                            dve.tensor_tensor(AG[s][:, g, :], OUT_T[:, :], RBS[:, :], ALU.mult).then_inc(*dve_attn.step(q))

                    for s in SLOTS:
                        statistics(it, 0, s)
                        normalise(it, 0, s)
                        x_lo(it, 0, s)
                    for s in SLOTS:
                        sums(it, 1, s)
                    statistics(it, 1, 0)
                    normalise(it, 1, 0)
                    x_lo(it, 1, 0)
                    statistics(it, 1, 1)
                    sums(it, 2, 0)
                    normalise(it, 1, 1)
                    x_lo(it, 1, 1)
                    sums(it, 2, 1)
                    for s, c in chunks:
                        dve.wait_ge(*pe_gram.at(it, (s, c)))
                        dve.scalar_tensor_tensor(out=GV[s][:, c, :], in0=work_bank(("gram", s, c))[:, :],
                                                               scalar=gram_c[:, c:c + 1], in1=AG[s][:, c, :],
                                                               op0=ALU.add, op1=ALU.mult).then_inc(*dve_gram.step((s, c)))
                    for k in range(HIDDEN[2]):
                        scaled_hidden(it, 0, k)
                    between = {1: (statistics, 2), 2: (normalise, 2), 3: (statistics, 3), 4: (normalise, 3)}
                    for k in range(HIDDEN[2]):
                        scaled_hidden(it, 1, k)
                        if k in between:
                            between[k][0](it, between[k][1], 0)
                    xn_transposed(it, 0)
                    statistics(it, 2, 1)
                    y_lo(it, 0, 0)
                    y_lo(it, 0, 1)
                    normalise(it, 2, 1)
                    statistics(it, 3, 1)
                    y_lo(it, 0, 2)
                    y_lo(it, 0, 3)
                    normalise(it, 3, 1)
                    pre_activation(it, 0)
                    xn_transposed(it, 1)
                    for b in range(NB):
                        y_lo(it, 1, b)
                    residual(it, 0)
                    statistics(it, 4, 0)
                    normalise(it, 4, 0)
                    pre_activation(it, 1)
                    residual(it, 1)
                    statistics(it, 4, 1)
                    normalise(it, 4, 1)

            @block.gpsimd
            def _(pool):
                def bias(it, L, s):
                    if L == 0:
                        for c in range(DC):
                            pool.wait_ge(*pe_xT.at(it, (s, c)))
                        src = RES[s]
                    else:
                        pool.wait_ge(*dve_norm.at(it, (L - 1, s, NB - 1)))
                        src = XN[s]
                    pool.tensor_tensor(RES[s][:, :, :], src[:, :, :],
                                                     b_rows[L][:, :].unsqueeze(1).to_broadcast([P, NB, D]), ALU.add).then_inc(*pool_res.step((L, s)))

                def rstd(it, L, s):
                    pool.compute_val(dve_aggr.at(it, (L, s, NB - 1))[1])
                    pool.wait_ge(i_sem, 4)
                    pool.wait_ge(*dve_aggr.at(it, (L, s, NB - 1)))
                    pool.tensor_scalar(VE[s][:, :], MV[s][:, :, 1], LN_EPS, None, ALU.add).then_inc(*pool_var.step((L, s)))
                    pool.wait_ge(*pool_var.at(it, (L, s)))
                    pool.tensor_tensor(RSTD[s][:, :], VE[s][:, :], neg_half[:, 0:NB], ALU.pow).then_inc(*pool_rstd.step((L, s)))

                def degrees(it, s):
                    pool.wait_ge(*act_adjT.at(it, (s, NB - 1)))
                    pool.compute_val(dve_din.at(it, s)[1])
                    pool.wait_ge(i_sem, 4)
                    pool.wait_ge(*dve_din.at(it, s))
                    pool.tensor_scalar(DNZ[s][:, :, :], DEG[s][:, :, :], 0.0, None, ALU.is_equal).then_inc(*pool_deg.step((s, 0)))
                    pool.compute_val(pool_deg.at(it, (s, 0))[1])
                    pool.wait_ge(i_sem, 4)
                    pool.wait_ge(*pool_deg.at(it, (s, 0)))
                    pool.tensor_tensor(DSC[s][:, :, :], DEG[s][:, :, :], DNZ[s][:, :, :], ALU.add).then_inc(*pool_deg.step((s, 1)))
                    pool.compute_val(pool_deg.at(it, (s, 1))[1])
                    pool.wait_ge(i_sem, 4)
                    pool.wait_ge(*pool_deg.at(it, (s, 1)))
                    pool.tensor_scalar(DNZ[s][:, :, :], DNZ[s][:, :, :], -1.0, 1.0, ALU.mult, ALU.add).then_inc(*pool_deg.step((s, 2)))
                    pool.tensor_tensor(DSC[s][:, :, :], DSC[s][:, :, :],
                                                     neg_half[:, :].rearrange("p (a b) -> p a b", a=2), ALU.pow).then_inc(*pool_deg.step((s, 3)))
                    pool.wait_ge(*pool_deg.at(it, (s, 3)))
                    pool.tensor_tensor(DRS[s][:, :, :], DSC[s][:, :, :], DNZ[s][:, :, :], ALU.mult).then_inc(*pool_deg.step((s, 4)))
                    pool.compute_val(pool_deg.at(it, (s, 4))[1])
                    pool.wait_ge(i_sem, 4)
                    pool.wait_ge(*pool_deg.at(it, (s, 4)))
                    pool.tensor_scalar(NSO[s][:, :], DRS[s][:, 0, :], -1.0, None, ALU.mult).then_inc(*pool_deg.step((s, 5)))

                with pool.Fori(1, PAIRS + 1) as it:
                    for s in SLOTS:
                        bias(it, 0, s)
                    for s in SLOTS:
                        degrees(it, s)
                    for L in (0, 1):
                        for s in SLOTS:
                            rstd(it, L, s)
                        for s in SLOTS:
                            bias(it, L + 1, s)
                    for L, s in ln_order[4:]:
                        rstd(it, L, s)


_INS = ['x', 'adj', 'L0_gnn_Wq', 'L0_gnn_bq', 'L0_gnn_Wk', 'L0_gnn_bk', 'L0_gnn_Wv', 'L0_gnn_bv', 'L0_gnn_Wo',
        'L0_gnn_bo', 'L1_gnn_eps', 'L1_gnn_W1', 'L1_gnn_b1', 'L1_gnn_W2', 'L1_gnn_b2', 'L2_gnn_epsilon',
        'L2_gnn_W1', 'L2_gnn_b1', 'L2_gnn_rms_weight', 'L2_gnn_W2', 'L2_gnn_b2', 'L3_gnn_gamma', 'L3_gnn_beta',
        'L3_gnn_W_self', 'L3_gnn_W_neigh']


def kernel(**inputs):
    import numpy as _np
    import concourse.bacc as _bacc
    from concourse import mybir as _mybir
    from concourse.bass_utils import run_bass_kernel_spmd as _run

    nc = _bacc.Bacc("TRN2", target_bir_lowering=False, num_devices=1)
    arrays, args = {}, []
    for name in _INS:
        a = _np.ascontiguousarray(inputs[name])
        if a.ndim == 0:
            a = a.reshape(1)
        arrays[f"in_{name}"] = a
        args.append(nc.dram_tensor(f"in_{name}", a.shape, _mybir.dt.from_np(a.dtype), kind="ExternalInput").ap())
    args.append(nc.dram_tensor("out", (N_GRAPHS, N, D), F32, kind="ExternalOutput").ap())
    build(nc, *args)
    r = _run(nc, [arrays], core_ids=[0])
    return r.results[0]["out"]
```

```python
from contextlib import ExitStack

import concourse.bass as bass
from concourse import mybir

ALU = mybir.AluOpType
ACT = mybir.ActivationFunctionType
AX = mybir.AxisListType
F32 = mybir.dt.float32
F32R = mybir.dt.float32r

P = 128
N_GRAPHS, N, D = 32, 512, 256
NB = N // P
DC = D // P
HEADS, HD = 8, 32
GH = P // HD
H1, H2 = 512, 1024
HIDDEN = {1: H1 // P, 2: H2 // P}
PAIRS = N_GRAPHS // 2
NEG = -9000000000000000.0
SLOTS = (0, 1)
LN_EPS = 1e-5
RMS_EPS = 1e-6

SEGMENTS = [(s, g) for g in range(HEADS // GH) for s in SLOTS]
SEG_TILES = NB * GH
TILES = SEG_TILES * len(SEGMENTS)
LAG = 3
STREAM = TILES + 9
WO_AT = (60, 61)
SCORE_BANKS, MASKED, PROBS = 3, 3, 4


def tile_of(i):
    s, g = SEGMENTS[i // SEG_TILES]
    return s, g, i % SEG_TILES // GH, i % GH


def qk_at(i):
    return {19: (0, 1, 0), 20: (0, 1, 1), 35: (1, 1, 0), 36: (1, 1, 1)}.get(i)


def segment_at(i, offset):
    q, r = divmod(i - offset, SEG_TILES)
    return q if r == 0 and 0 <= q < len(SEGMENTS) else None


class Signal:

    def __init__(self, sem, keys, by=1, ahead=()):
        keys = [k for k in keys if k not in ahead] + list(ahead)
        self.credit = (len(keys) - len(ahead)) * by
        self.sem, self.by, self.total = sem, by, len(keys) * by
        self.place = {k: (n + 1) * by for n, k in enumerate(keys)}
        self.keys, self.next = list(keys), len(keys) - len(ahead)

    def step(self, key):
        assert self.keys[self.next % len(self.keys)] == key, (key, self.keys[self.next % len(self.keys)])
        self.next += 1
        return self.sem, self.by

    def at(self, it, key, turns_back=0):
        return self.sem, it * self.total + (self.place[key] - turns_back * self.total)


def build(nc, x, adj, Wq, bq, Wk, bk, Wv, bv, Wo, bo, eps1, W1, b1, W2, b2,
          eps2, V1, c1, rms_w, V2, c2, gamma, beta, W_self, W_neigh, out):
    ctx = ExitStack()
    with ctx:
        def sb(name, shape, dt=F32):
            return ctx.enter_context(nc.sbuf_tensor(name, shape, dt))

        ident = sb("ident", [P, P])
        ones = sb("ones", [P, P])
        neg_half = sb("neg_half", [P, 8])
        diag = {1: sb("diag1", [P, P]), 2: sb("diag2", [P, P])}
        wq, wk, wv, wo = (sb(n, [P, DC, D]) for n in ("wq", "wk", "wv", "wo"))
        w_up = {1: sb("w1", [P, DC, H1]), 2: sb("v1", [P, DC, H2])}
        w_down = {1: sb("w2", [P, HIDDEN[1], D]), 2: sb("v2", [P, HIDDEN[2], D])}
        w_cat = sb("w_cat", [P, DC, 2 * D])
        gram = sb("gram", [P, DC, D])
        bqk = sb("bqk", [P, 2, DC])
        b_up = {1: sb("b1c", [P, HIDDEN[1]]), 2: sb("c1c", [P, HIDDEN[2]])}
        rms = sb("rms", [P, HIDDEN[2]])
        gb = sb("gb", [P, 2, DC])
        bv_rows = sb("bv_rows", [P, D])
        b_rows = {0: sb("bo_rows", [P, D]), 1: sb("b2_rows", [P, D]), 2: sb("c2_rows", [P, D])}
        eps_col = sb("eps_col", [P, 2])
        gram_c = sb("gram_c", [P, DC])
        sq_eps = sb("sq_eps", [P, 1])
        small = sb("small", [P, 16])

        def two(name, shape, dt=F32):
            return [sb(f"{name}{s}", shape, dt) for s in SLOTS]

        RES = two("res", [P, NB, D])
        XN = two("xn", [P, NB, D])
        ADJ = two("adj", [P, NB, N])
        ADJT = two("adjT", [P, NB, N], F32R)
        XT = two("xT", [P, DC, N])
        AG = two("ag", [P, DC, N])
        VN = two("vn", [P, NB, D])
        STK = two("stk", [P, 2, GH, N], F32R)
        STG = [sb(f"stg{w}", [P, 2, N], F32R) for w in range(2)]
        PT = sb("pT", [P, 2, GH, NB, 2 * P])
        SM = sb("masked", [P, MASKED, N])
        PR = sb("probs", [P, PROBS, N])
        REXP = sb("rexp", [P, N])
        RBS = sb("rbs", [P, N])
        NMAX = sb("nmax", [P, MASKED])
        RS = sb("rs", [P, 2, SEG_TILES])
        RR = sb("rr", [P, SEG_TILES])
        STATS = two("stats", [P, NB, 6])
        MV = two("mv", [P, NB, 2])
        VE = two("ve", [P, NB])
        RSTD = two("rstd", [P, NB])
        DEG = two("deg", [P, 2, NB])
        DNZ = two("dnz", [P, 2, NB])
        DSC = two("dsc", [P, 2, NB])
        DRS = two("drs", [P, 2, NB])
        NSO = two("nso", [P, NB])
        XH = [STK[s][:, 0, 0:2, :].rearrange("p a (b d) -> p (a b) d", d=D) for s in SLOTS]
        XL = [STK[s][:, 0, 2:4, :].rearrange("p a (b d) -> p (a b) d", d=D) for s in SLOTS]
        HB = [PT[:, 0, n, 0:2, :].rearrange("p a b -> p (a b)") for n in range(3)]
        ZB = [PT[:, 0, n, 2:4, :].rearrange("p a b -> p (a b)") for n in range(2)]
        RMSB = [REXP[:, :], RBS[:, :]]
        PA = [AG[s][:, :, :].rearrange("p c (b d) -> p (c b) d", d=D) for s in SLOTS]
        TMP = [XT[s][:, :, :].rearrange("p c (b d) -> p (c b) d", d=D) for s in SLOTS]
        GV = [VN[s][:, :, :].rearrange("p (c b) d -> p c (b d)", c=DC) for s in SLOTS]

        banks = [ctx.enter_context(nc.psum_tensor(f"bank{n}", [P, N], F32)) for n in range(8)]
        ACC = banks[4:8]
        OUT_T = banks[7]

        w_sem = ctx.enter_context(nc.semaphore("weights_loaded"))
        v_sem = ctx.enter_context(nc.semaphore("hidden_weights_loaded"))
        i_sem = ctx.enter_context(nc.semaphore("ident_ready"))
        t_sem = ctx.enter_context(nc.semaphore("v1T_in_psum"))
        u_sem = ctx.enter_context(nc.semaphore("v1T_copied"))
        g_sem = ctx.enter_context(nc.semaphore("gram_in_psum"))
        k_sem = ctx.enter_context(nc.semaphore("constants_done"))
        V1T = PT[:, 0, :, :, :].rearrange("p a b c -> p (a b c)").rearrange("p (k d) -> p k d", d=D)[:, 0:HIDDEN[2], :]

        def rows_to_all(v):
            return v.rearrange("(a n) -> a n", a=1)[0:1, :].to_broadcast([P, v.shape[0]])

        with nc.Block() as setup:
            @setup.sync
            def _(sp):
                sp.dma_start(w_up[2][:, :, :], V1.rearrange("(c p) n -> p c n", p=P)).then_inc(v_sem, 16)
                sp.dma_start(b_up[2][:, :], c1.rearrange("(c p) -> p c", p=P), allow_slow_non_contiguous=True).then_inc(v_sem, 16)
                n = 0
                for dst, src in ((wq, Wq), (wk, Wk), (wv, Wv), (wo, Wo), (w_up[1], W1)):
                    sp.dma_start(dst[:, :, :], src.rearrange("(c p) n -> p c n", p=P)).then_inc(w_sem, 16)
                for dst, src in ((w_down[1], W2), (w_down[2], V2)):
                    sp.dma_start(dst[:, :, :], src.rearrange("(c p) n -> p c n", p=P)).then_inc(w_sem, 16)
                for h, src in enumerate((W_self, W_neigh)):
                    sp.dma_start(w_cat[:, :, h * D:(h + 1) * D], src.rearrange("(c p) n -> p c n", p=P)).then_inc(w_sem, 16)
                for dst, src in ((bqk[:, 0, :], bq), (bqk[:, 1, :], bk), (b_up[1][:, :], b1), (rms[:, :], rms_w),
                                 (gb[:, 0, :], gamma), (gb[:, 1, :], beta)):
                    sp.dma_start(dst, src.rearrange("(c p) -> p c", p=P), allow_slow_non_contiguous=True).then_inc(w_sem, 16)
                for dst, src in ((bv_rows[:, :], bv), (b_rows[0][:, :], bo),
                                 (b_rows[1][:, :], b2), (b_rows[2][:, :], c2),
                                 (eps_col[:, 0:1], eps1), (eps_col[:, 1:2], eps2)):
                    sp.dma_start(dst, rows_to_all(src)).then_inc(w_sem, 16)
                sp.wait_ge(w_sem, 16 * 21)
                sp.wait_ge(v_sem, 32)

            @setup.gpsimd
            def _(pool):
                pool.memset(ident[:, :], 0.0).then_inc(i_sem, 1)
                pool.wait_ge(i_sem, 1)
                pool.affine_select(out=ident[:, :], in_=ident[:, :], compare_op=ALU.not_equal, fill=1.0,
                                   base=0, pattern=[[-1, P]], channel_multiplier=1).then_inc(i_sem, 1)
                pool.memset(ones[:, :], 1.0 / H2).then_inc(i_sem, 1)
                pool.memset(neg_half[:, :], -0.5).then_inc(i_sem, 1)
                pool.wait_ge(i_sem, 4)

            @setup.tensor
            def _(pe):
                pe.wait_ge(i_sem, 4)
                pe.wait_ge(v_sem, 32)
                for k in range(HIDDEN[2]):
                    for c in range(DC):
                        last = pe.transpose(banks[k // 2][:, (k % 2) * D + c * P:(k % 2) * D + (c + 1) * P],
                                            w_up[2][:, c, k * P:(k + 1) * P], ident[:, :])
                last.then_inc(t_sem, 1)
                pe.wait_ge(u_sem, 5)
                for c in range(DC):
                    for k in range(HIDDEN[2]):
                        pe.matmul(banks[4 + c][:, 0:D], V1T[:, k, c * P:(c + 1) * P], V1T[:, k, :],
                                  start=k == 0, stop=k == HIDDEN[2] - 1)
                    for k in range(HIDDEN[2]):
                        last = pe.matmul(banks[6 + c][:, 0:1], V1T[:, k, c * P:(c + 1) * P], b_up[2][:, k:k + 1],
                                         start=k == 0, stop=k == HIDDEN[2] - 1)
                last = pe.matmul(banks[0][:, 0:1], ones[:, :], small[:, 0:1], start=True, stop=True)
                last.then_inc(g_sem, 1)

            @setup.vector
            def _(dve):
                dve.wait_ge(t_sem, 1)
                for b in range(4):
                    dve.tensor_copy(V1T[:, 2 * b:2 * b + 2, :],
                                    banks[b][:, :].rearrange("p (k d) -> p k d", d=D)).then_inc(u_sem, 1)
                dve.tensor_tensor_reduce(small[:, 8:16], b_up[2][:, :], b_up[2][:, :], 1.0, 0.0, ALU.mult, ALU.add,
                                         small[:, 0:1]).then_inc(u_sem, 1)
                dve.wait_ge(w_sem, 16 * 21)
                dve.tensor_tensor(w_cat[:, :, 0:D], w_cat[:, :, 0:D], w_cat[:, :, D:2 * D], ALU.add).then_inc(k_sem, 1)
                dve.scalar_tensor_tensor(out=diag[1][:, :], in0=ident[:, :], scalar=eps_col[:, 0:1], in1=ident[:, :],
                                         op0=ALU.mult, op1=ALU.add).then_inc(k_sem, 1)
                dve.tensor_scalar(diag[2][:, :], ident[:, :], eps_col[:, 1:2], None, ALU.mult).then_inc(k_sem, 1)
                dve.wait_ge(g_sem, 1)
                for c in range(DC):
                    dve.tensor_copy(gram[:, c, :], banks[4 + c][:, 0:D]).then_inc(k_sem, 1)
                    dve.tensor_scalar(gram_c[:, c:c + 1], banks[6 + c][:, 0:1], 2.0, None, ALU.mult).then_inc(k_sem, 1)
                dve.tensor_scalar(sq_eps[:, :], banks[0][:, 0:1], RMS_EPS, None, ALU.add).then_inc(k_sem, 1)
                dve.wait_ge(k_sem, 8)

        signals = []

        def signal(name, keys, by=1, ahead=()):
            s = Signal(ctx.enter_context(nc.semaphore(name)), keys, by, ahead)
            signals.append(s)
            return s

        chunks = [(s, c) for s in SLOTS for c in range(DC)]
        blocks = [(s, b) for s in SLOTS for b in range(NB)]
        qk1, qk0 = ([(s, g, w) for s in SLOTS for w in range(2)] for g in (1, 0))
        hids = [(L, s, k) for L in (1, 2) for s in SLOTS for k in range(HIDDEN[L])]
        tiles = list(range(TILES))
        acc_blocks = [(0, s, h) for s in SLOTS for h in range(2)] + [(L, s, b) for L in (1, 2) for s, b in blocks]
        norms = [(0, 0), (0, 1), (1, 0), (1, 1), (2, 0), (3, 0), (2, 1), (3, 1), (4, 0), (4, 1)]
        norm_blocks = [(L, s, b) for L, s in norms for b in range(NB)]

        x_loaded = [signal(f"x_loaded{s}", [], 16, ahead=["x"]) for s in SLOTS]
        adj_loaded = [signal(f"adj_loaded{s}", [], 16, ahead=["adj"]) for s in SLOTS]
        spilled = [signal(f"spilled{w}", [(s, 1) for s in SLOTS], 16, ahead=[(s, 0) for s in SLOTS]) for w in range(2)]
        stacked = [[signal(f"stacked{s}{w}", [(1, r) for r in range(4)], 16, ahead=[(0, r) for r in range(4)])
                    for w in range(2)] for s in SLOTS]
        stored = [signal(f"stored{s}", ["out"], 16) for s in SLOTS]

        pe_xT = signal("pe_xT", [], ahead=chunks)
        pe_adjT = signal("pe_adjT", [], ahead=blocks)
        pe_qk = signal("pe_qk", qk1, ahead=qk0)
        pe_v = signal("pe_v", [], ahead=chunks)
        pe_scores = signal("pe_scores", tiles)
        pe_pT = signal("pe_pT", tiles)
        pe_av = signal("pe_av", range(TILES // 8))
        pe_rb = signal("pe_rb", range(4))
        pe_wo = signal("pe_wo", chunks)
        pe_agg = signal("pe_agg", [(L, s, c) for L in (1, 2) for s, c in chunks])
        pe_hid = signal("pe_hid", hids)
        pe_used = signal("pe_used", hids)
        pe_gram = signal("pe_gram", chunks)
        pe_ms = signal("pe_ms", SLOTS)
        pe_xnT = signal("pe_xnT", chunks)
        pe_p1 = signal("pe_p1", blocks)
        pe_z = signal("pe_z", SLOTS)

        act_adjT = signal("act_adjT", [], ahead=blocks)
        act_hi = signal("act_hi", qk1, ahead=qk0)
        act_exp = signal("act_exp", tiles)
        act_pT = signal("act_pT", [i for i in tiles if i % 2])
        act_rb = signal("act_rb", range(4))
        act_xh = signal("act_xh", [(L, s) for L in range(2) for s in SLOTS])
        act_agg = signal("act_agg", [(L, s) for L in (1, 2) for s in SLOTS])
        act_hid = signal("act_hid", hids)
        act_rms = signal("act_rms", [(s, n) for s in SLOTS for n in range(2)])
        act_p1 = signal("act_p1", blocks)
        act_soft = signal("act_soft", [(s, n) for s in SLOTS for n in range(3)])

        dve_xT = signal("dve_xT", [], ahead=chunks)
        dve_din = signal("dve_din", [], ahead=SLOTS)
        dve_lo = signal("dve_lo", qk1, ahead=qk0)
        dve_mask = signal("dve_mask", [], ahead=SLOTS)
        dve_v = signal("dve_v", [], ahead=chunks)
        dve_max = signal("dve_max", tiles)
        dve_pT = signal("dve_pT", [i for i in tiles if i % 2 == 0])
        dve_recip = signal("dve_recip", [(q, n) for q in range(4) for n in range(2)])
        dve_attn = signal("dve_attn", range(4))
        dve_add = signal("dve_add", acc_blocks)
        dve_stat = signal("dve_stat", norm_blocks)
        dve_aggr = signal("dve_aggr", norm_blocks)
        dve_norm = signal("dve_norm", norm_blocks)
        dve_xl = signal("dve_xl", [(L, s) for L in range(2) for s in SLOTS])
        dve_agg = signal("dve_agg", [(L, s) for L in (1, 2) for s in SLOTS])
        dve_gram = signal("dve_gram", chunks)
        dve_z = signal("dve_z", [(s, k) for s in SLOTS for k in range(HIDDEN[2])])
        dve_xnT = signal("dve_xnT", chunks)
        dve_yl = signal("dve_yl", blocks)
        dve_pre = signal("dve_pre", blocks)
        dve_soft = signal("dve_soft", [(s, n) for s in SLOTS for n in range(2)])

        pool_res = signal("pool_res", [(L, s) for L in (1, 2) for s in SLOTS], ahead=[(0, s) for s in SLOTS])
        pool_var = signal("pool_var", norms)
        pool_rstd = signal("pool_rstd", norms)
        pool_deg = signal("pool_deg", [], ahead=[(s, n) for s in SLOTS for n in range(6)])

        work = []
        for i in range(STREAM):
            t = i - LAG
            if 0 <= t < TILES:
                work.append((("pT", t), act_pT if t % 2 else dve_pT, t))
            if qk_at(i):
                work.append((("qk", *qk_at(i)), dve_lo, qk_at(i)))
            if (q := segment_at(i, 21)) is not None:
                work.append((("rb", q), act_rb, q))
            if i in WO_AT:
                work.append((("wo", 0, WO_AT.index(i)), dve_add, (0, 0, WO_AT.index(i))))
        work += [(("wo", 1, h), dve_add, (0, 1, h)) for h in range(2)]

        def work_agg(L, s):
            return [(("agg", L, s, c), act_agg if c == 0 else dve_agg, (L, s)) for c in range(DC)]

        def work_hid(L, s):
            return [(("hid", L, s, k), *((act_hid, (L, s, k)) if L == 1 else (dve_z, (s, k)))) for k in range(HIDDEN[L])]

        def work_gram(s):
            return [(("gram", s, c), dve_gram, (s, c)) for c in range(DC)]

        def work_ms(s):
            return [(("ms", s), act_rms, (s, 0))]

        def work_xnT(s):
            return [(("xnT", s, c), dve_xnT, (s, c)) for c in range(DC)]

        def work_p1(s):
            return [(("p1", s, b), dve_yl, (s, b)) for b in range(NB)]

        def work_xT(s):
            return [(("xT", s, c), dve_xT, (s, c)) for c in range(DC)]

        def work_adjT(s):
            return [(("adjT", s, b), act_adjT, (s, b)) for b in range(NB)]

        def work_qkv(s):
            return ([(("qk", s, 0, w), dve_lo, (s, 0, w)) for w in range(2)]
                    + [(("v", s, h), dve_v, (s, h)) for h in range(2)])

        work += work_agg(1, 0) + work_hid(1, 0) + work_agg(1, 1) + work_hid(1, 1)
        work += work_agg(2, 0) + work_gram(0) + work_agg(2, 1) + work_ms(0) + work_gram(1) + work_ms(1)
        work += work_hid(2, 0) + work_hid(2, 1)
        work += work_xnT(0) + work_p1(0) + work_xnT(1) + work_p1(1)
        entry_starts = len(work)
        work += work_xT(0) + work_adjT(0) + work_qkv(0) + work_xT(1) + work_adjT(1) + work_qkv(1)
        while len(work) % 4:
            work.append((None, None, None))
        place = {w[0]: n for n, w in enumerate(work)}

        def work_bank(key):
            return banks[place[key] % 4]

        def bank_read(it, key):
            n, back = place[key] - 4, 0
            while n < 0 or work[n][0] is None:
                if n < 0:
                    n, back = n + len(work), 1
                else:
                    n -= 4
            return work[n][1].at(it, work[n][2], back)

        x_v = x.rearrange("g (t p) d -> g p t d", p=P)
        adj_v = adj.rearrange("g (t p) m -> g p t m", p=P)
        out_v = out.rearrange("g (t p) d -> g p t d", p=P)
        scratch = [[nc.dram_tensor(f"qk_parts{s}{w}", (2, P, N), F32).ap() for w in range(2)] for s in SLOTS]

        with nc.Block() as block:
            @block.sync
            def _(sp):
                def stack(it, s, g):
                    for w in range(2):
                        if not (g == 0 and type(it) is int):
                            sp.compute_val(dve_lo.at(it, (s, g, w))[1])
                            sp.wait_ge(*stacked[s][w].at(it, (1 - g, 3), g))
                        sp.wait_ge(*dve_lo.at(it, (s, g, w)))
                        sp.dma_start(scratch[s][w].rearrange("a p n -> p a n"),
                                     STG[w][:, :, :].bitcast(F32)).then_inc(*spilled[w].step((s, g)))
                    if g:
                        sp.wait_ge(*pe_scores.at(it, SEG_TILES * SEGMENTS.index((s, 0)) + SEG_TILES - 1))
                    else:
                        sp.wait_ge(*pe_z.at(it, s))
                    for w in range(2):
                        sp.wait_ge(*spilled[w].at(it, (s, g)))
                        for r in range(4):
                            part = r % 2 if w == 0 else r // 2
                            sp.dma_start(STK[s][r * HD:(r + 1) * HD, w, :, :].bitcast(F32),
                                         scratch[s][w][part].rearrange("(j p) n -> p j n", p=HD)
                                         ).then_inc(*stacked[s][w].step((g, r)))

                for s in signals:
                    if s.credit:
                        sp.sem_inc(s.sem, s.credit)
                for s in SLOTS:
                    sp.dma_start(RES[s][:, :, :], x_v[s]).then_inc(*x_loaded[s].step("x"))
                for s in SLOTS:
                    sp.dma_start(ADJ[s][:, :, :], adj_v[s]).then_inc(*adj_loaded[s].step("adj"))
                for s in SLOTS:
                    stack(0, s, 0)
                with sp.Fori(1, PAIRS + 1) as it:
                    pair = sp.snap(it & (PAIRS - 1))
                    following = [sp.snap(pair * 2 + s) for s in SLOTS]
                    present = [sp.snap(it * 2 + (s - 2)) for s in SLOTS]
                    for s in SLOTS:
                        sp.compute_val(following[s])
                        sp.compute_val(present[s])
                    for s in SLOTS:
                        stack(it, s, 1)
                    for s in SLOTS:
                        sp.wait_ge(*dve_max.at(it, SEG_TILES * SEGMENTS.index((s, 1)) + SEG_TILES - 1))
                        sp.dma_start(ADJ[s][:, :, :], adj_v[following[s]]).then_inc(*adj_loaded[s].step("adj"))
                    for s in SLOTS:
                        sp.wait_ge(*dve_norm.at(it, (2, s, NB - 1)))
                        sp.dma_start(RES[s][:, :, :], x_v[following[s]]).then_inc(*x_loaded[s].step("x"))
                    for s in SLOTS:
                        sp.wait_ge(*dve_norm.at(it, (4, s, NB - 1)))
                        sp.dma_start(out_v[present[s]], VN[s][:, :, :]).then_inc(*stored[s].step("out"))
                        stack(it, s, 0)
                for s in SLOTS:
                    sp.wait_ge(stored[s].sem, stored[s].total * (PAIRS + 1))
                    sp.wait_ge(x_loaded[s].sem, x_loaded[s].total * (PAIRS + 1))
                    sp.wait_ge(adj_loaded[s].sem, adj_loaded[s].total * (PAIRS + 1))
                    for w in range(2):
                        sp.wait_ge(stacked[s][w].sem, stacked[s][w].total * (PAIRS + 1))
                for w in range(2):
                    sp.wait_ge(spilled[w].sem, spilled[w].total * (PAIRS + 1))

            @block.tensor
            def _(pe):
                def project_qk(it, s, g, w):
                    bank = work_bank(("qk", s, g, w))
                    pe.wait_ge(*bank_read(it, ("qk", s, g, w)))
                    for c in range(DC):
                        last = pe.matmul(bank[:, :], (wq, wk)[w][:, c, g * P:(g + 1) * P], XT[s][:, c, :],
                                         start=c == 0, stop=c == DC - 1)
                    last.then_inc(*pe_qk.step((s, g, w)))

                def transpose_x(it, s):
                    pe.wait_ge(*x_loaded[s].at(it, "x"))
                    for c in range(DC):
                        bank = work_bank(("xT", s, c))
                        pe.wait_ge(*bank_read(it, ("xT", s, c)))
                        for b in range(NB):
                            last = pe.transpose(bank[:, b * P:(b + 1) * P], RES[s][:, b, c * P:(c + 1) * P], ident[:, :])
                        last.then_inc(*pe_xT.step((s, c)))

                def transpose_adj(it, s):
                    pe.wait_ge(*adj_loaded[s].at(it, "adj"))
                    for m in range(NB):
                        bank = work_bank(("adjT", s, m))
                        pe.wait_ge(*bank_read(it, ("adjT", s, m)))
                        for b in range(NB):
                            last = pe.transpose(bank[:, b * P:(b + 1) * P], ADJ[s][:, b, m * P:(m + 1) * P], ident[:, :])
                        last.then_inc(*pe_adjT.step((s, m)))

                def first_qkv(it, s):
                    pe.wait_ge(*dve_xT.at(it, (s, DC - 1)))
                    for w in range(2):
                        project_qk(it, s, 0, w)
                    for half in range(2):
                        bank = work_bank(("v", s, half))
                        pe.wait_ge(*bank_read(it, ("v", s, half)))
                        for b in range(2):
                            for c in range(DC):
                                nb = 2 * half + b
                                last = pe.matmul(bank[:, b * D:(b + 1) * D], XT[s][:, c, nb * P:(nb + 1) * P],
                                                 wv[:, c, :], start=c == 0, stop=c == DC - 1)
                        last.then_inc(*pe_v.step((s, half)))

                def project_out(it, s, half):
                    bank = work_bank(("wo", s, half))
                    pe.wait_ge(*bank_read(it, ("wo", s, half)))
                    pe.wait_ge(*dve_attn.at(it, 2 + s))
                    for b in range(2):
                        nb = 2 * half + b
                        for c in range(DC):
                            last = pe.matmul(bank[:, b * D:(b + 1) * D], AG[s][:, c, nb * P:(nb + 1) * P], wo[:, c, :],
                                             start=c == 0, stop=c == DC - 1)
                    last.then_inc(*pe_wo.step((s, half)))

                def neighbour_sums(it, L, s):
                    pe.wait_ge(*act_adjT.at(it, (s, NB - 1), 1))
                    pe.wait_ge(*dve_xl.at(it, (L - 1, s)))
                    for c in range(DC):
                        bank = work_bank(("agg", L, s, c))
                        pe.wait_ge(*bank_read(it, ("agg", L, s, c)))
                        for m in range(NB):
                            for n, part in enumerate((XH, XL)):
                                pe.matmul(bank[:, :], part[s][:, m, c * P:(c + 1) * P], ADJT[s][:, m, :],
                                          start=m == 0 and n == 0, stop=False)
                        for m in range(NB):
                            last = pe.matmul(bank[:, m * P:(m + 1) * P], XN[s][:, m, c * P:(c + 1) * P], diag[L][:, :],
                                             start=False, stop=m == NB - 1)
                        last.then_inc(*pe_agg.step((L, s, c)))

                def mlp(it, L, s):
                    pe.wait_ge(*act_agg.at(it, (L, s)))
                    pe.wait_ge(*dve_agg.at(it, (L, s)))
                    for k in range(HIDDEN[L] + 2):
                        if k < HIDDEN[L]:
                            bank = work_bank(("hid", L, s, k))
                            pe.wait_ge(*bank_read(it, ("hid", L, s, k)))
                            for c in range(DC):
                                last = pe.matmul(bank[:, :], w_up[L][:, c, k * P:(k + 1) * P], AG[s][:, c, :],
                                                 start=c == 0, stop=c == DC - 1)
                            last.then_inc(*pe_hid.step((L, s, k)))
                        if k >= 2:
                            h = k - 2
                            if h == 0:
                                if (L, s) == (1, 0):
                                    pe.wait_ge(*dve_max.at(it, TILES - 1))
                                    pe.wait_ge(*dve_attn.at(it, 3))
                                else:
                                    pe.wait_ge(*dve_add.at(it, (L, 0, NB - 1) if s else (L - 1, 1, NB - 1)))
                            pe.wait_ge(*act_hid.at(it, (L, s, h)))
                            slot = hids.index((L, s, h)) % 3
                            for b in range(NB):
                                last = pe.matmul(ACC[b][:, 0:D], HB[slot][:, b * P:(b + 1) * P], w_down[L][:, h, :],
                                                 start=h == 0, stop=h == HIDDEN[L] - 1)
                            last.then_inc(*pe_used.step((L, s, h)))

                def gram_product(it, s):
                    pe.wait_ge(*act_agg.at(it, (2, s)))
                    pe.wait_ge(*dve_agg.at(it, (2, s)))
                    for c in range(DC):
                        bank = work_bank(("gram", s, c))
                        pe.wait_ge(*bank_read(it, ("gram", s, c)))
                        for e in range(DC):
                            last = pe.matmul(bank[:, :], gram[:, e, c * P:(c + 1) * P], AG[s][:, e, :],
                                             start=e == 0, stop=e == DC - 1)
                        last.then_inc(*pe_gram.step((s, c)))

                def mean_square(it, s):
                    bank = work_bank(("ms", s))
                    pe.wait_ge(*bank_read(it, ("ms", s)))
                    for c in range(DC):
                        pe.wait_ge(*dve_gram.at(it, (s, c)))
                        last = pe.matmul(bank[:, :], ones[:, :], GV[s][:, c, :], start=c == 0, stop=c == DC - 1)
                    last.then_inc(*pe_ms.step(s))

                def transpose_xn(it, s):
                    pe.wait_ge(*dve_norm.at(it, (3, s, NB - 1)))
                    for c in range(DC):
                        bank = work_bank(("xnT", s, c))
                        pe.wait_ge(*bank_read(it, ("xnT", s, c)))
                        for b in range(NB):
                            last = pe.transpose(bank[:, b * P:(b + 1) * P], VN[s][:, b, c * P:(c + 1) * P], ident[:, :])
                        last.then_inc(*pe_xnT.step((s, c)))

                def both_weights(it, s):
                    for b in range(NB):
                        bank = work_bank(("p1", s, b))
                        pe.wait_ge(*bank_read(it, ("p1", s, b)))
                        pe.wait_ge(*dve_xnT.at(it, (s, DC - 1)))
                        for c in range(DC):
                            last = pe.matmul(bank[:, :], XT[s][:, c, b * P:(b + 1) * P], w_cat[:, c, :],
                                             start=c == 0, stop=c == DC - 1)
                        last.then_inc(*pe_p1.step((s, b)))

                def adj_y(it, s):
                    pe.wait_ge(*(dve_pre.at(it, (0, NB - 1)) if s else dve_add.at(it, (2, 1, NB - 1))))
                    pe.wait_ge(*dve_yl.at(it, (s, NB - 1)))
                    for b in range(NB):
                        for m in range(NB):
                            for n, part in enumerate((XH, XL)):
                                last = pe.matmul(ACC[b][:, 0:D], ADJT[s][:, m, b * P:(b + 1) * P], part[s][:, m, :],
                                                 start=m == 0 and n == 0, stop=m == NB - 1 and n == 1)
                    last.then_inc(*pe_z.step(s))

                transpose_x(0, 0)
                transpose_adj(0, 0)
                first_qkv(0, 0)
                transpose_x(0, 1)
                transpose_adj(0, 1)
                first_qkv(0, 1)

                with pe.Fori(1, PAIRS + 1) as it:
                    for i in range(STREAM):
                        if i < TILES:
                            s, g, b, j = tile_of(i)
                            if i % SEG_TILES == 0:
                                for w in range(2):
                                    pe.wait_ge(*stacked[s][w].at(it, (g, 3), 1 - g))
                            if i < SCORE_BANKS:
                                pe.wait_ge(*dve_pre.at(it, (1, NB - 1), 1))
                            else:
                                pe.wait_ge(*dve_max.at(it, i - SCORE_BANKS))
                            pe.matmul(banks[4 + i % SCORE_BANKS][:, :], STK[s][:, 0, j, b * P:(b + 1) * P],
                                      STK[s][:, 1, j, :], start=True, stop=True).then_inc(*pe_scores.step(i))
                        t = i - LAG
                        if 0 <= t < TILES:
                            bank = work_bank(("pT", t))
                            pe.wait_ge(*bank_read(it, ("pT", t)))
                            pe.wait_ge(*act_exp.at(it, t))
                            for k in range(NB):
                                last = pe.transpose(bank[:, k * P:(k + 1) * P], PR[:, t % PROBS, k * P:(k + 1) * P], ident[:, :])
                            last.then_inc(*pe_pT.step(t))
                        if qk_at(i):
                            project_qk(it, *qk_at(i))
                        p, k = divmod(i - 12, 8)
                        if k < NB and 0 <= p < TILES // 8:
                            s, g, b, _ = tile_of(8 * p)
                            if k == 0:
                                pe.wait_ge(*act_pT.at(it, 8 * p + 7))
                                pe.wait_ge(*dve_pT.at(it, 8 * p + 6))
                                pe.wait_ge(*dve_v.at(it, (s, DC - 1), 1))
                                if p == 0:
                                    pe.wait_ge(*dve_pre.at(it, (1, NB - 1), 1))
                                elif p % 2 == 0:
                                    pe.wait_ge(*dve_attn.at(it, p // 2 - 1))
                            for j in range(GH):
                                h = g * GH + j
                                last = pe.matmul(OUT_T[j * HD:(j + 1) * HD, b * P:(b + 2) * P],
                                                 VN[s][:, k, h * HD:(h + 1) * HD], PT[:, p % 2, j, k, :],
                                                 start=k == 0, stop=k == NB - 1)
                            if k == NB - 1:
                                last.then_inc(*pe_av.step(p))
                        if (q := segment_at(i, 21)) is not None:
                            bank = work_bank(("rb", q))
                            pe.wait_ge(*bank_read(it, ("rb", q)))
                            pe.wait_ge(*dve_recip.at(it, (q, 1)))
                            for b in range(NB):
                                last = pe.transpose(bank[:, b * P:(b + 1) * P], REXP[:, b * P:(b + 1) * P], ident[:, :])
                            last.then_inc(*pe_rb.step(q))
                        if i in WO_AT:
                            project_out(it, 0, WO_AT.index(i))
                    for half in range(2):
                        project_out(it, 1, half)

                    for s in SLOTS:
                        neighbour_sums(it, 1, s)
                        mlp(it, 1, s)

                    neighbour_sums(it, 2, 0)
                    gram_product(it, 0)
                    neighbour_sums(it, 2, 1)
                    mean_square(it, 0)
                    gram_product(it, 1)
                    mean_square(it, 1)
                    mlp(it, 2, 0)
                    mlp(it, 2, 1)

                    transpose_xn(it, 0)
                    both_weights(it, 0)
                    adj_y(it, 0)
                    transpose_xn(it, 1)
                    both_weights(it, 1)
                    transpose_x(it, 0)
                    transpose_adj(it, 0)
                    adj_y(it, 1)
                    first_qkv(it, 0)
                    transpose_x(it, 1)
                    transpose_adj(it, 1)
                    first_qkv(it, 1)

            @block.scalar
            def _(act):
                def hi_part(it, s, g, w):
                    before = (0, g) if s else (1, 1 - g)
                    if not (type(it) is int and s == 0):
                        act.wait_ge(*spilled[w].at(it, before, 1 if (s, g) == (0, 1) else 0))
                    act.wait_ge(*pe_qk.at(it, (s, g, w)))
                    act.activation(STG[w][:, 0, :], work_bank(("qk", s, g, w))[:, :], ACT.Identity,
                                   bias=bqk[:, w, g:g + 1]).then_inc(*act_hi.step((s, g, w)))

                def keep_adjT(it, s):
                    for m in range(NB):
                        if m == 0:
                            act.wait_ge(*pe_z.at(it, s))
                            if type(it) is not int:
                                act.wait_ge(*pool_deg.at(it, (s, 5), 1))
                        act.wait_ge(*pe_adjT.at(it, (s, m)))
                        act.activation(ADJT[s][:, m, :], work_bank(("adjT", s, m))[:, :], ACT.Copy,
                                       accum_out=DEG[s][:, 0, m:m + 1]).then_inc(*act_adjT.step((s, m)))

                def x_hi(it, L, s):
                    act.wait_ge(*dve_norm.at(it, (L, s, NB - 1)))
                    act.activation(XH[s], XN[s][:, :, :], ACT.Copy).then_inc(*act_xh.step((L, s)))

                def sums(it, L, s):
                    act.wait_ge(*pe_agg.at(it, (L, s, 0)))
                    act.activation(AG[s][:, 0, :], work_bank(("agg", L, s, 0))[:, :], ACT.Copy).then_inc(*act_agg.step((L, s)))

                def hidden(it, L, s, k):
                    n = hids.index((L, s, k))
                    if n >= 3:
                        act.wait_ge(*pe_used.at(it, hids[n - 3]))
                    if L == 1:
                        act.wait_ge(*pe_hid.at(it, (1, s, k)))
                        act.activation(HB[n % 3], work_bank(("hid", 1, s, k))[:, :], ACT.Relu,
                                       bias=b_up[1][:, k:k + 1]).then_inc(*act_hid.step((1, s, k)))
                    else:
                        act.wait_ge(*dve_z.at(it, (s, k)))
                        act.activation(HB[n % 3], ZB[k % 2], ACT.Silu,
                                       scale=rms[:, k:k + 1]).then_inc(*act_hid.step((2, s, k)))

                def inverse_rms(it, s):
                    act.wait_ge(*pe_ms.at(it, s))
                    act.activation(RMSB[s], work_bank(("ms", s))[:, :], ACT.Ln, bias=sq_eps[:, :]).then_inc(*act_rms.step((s, 0)))
                    act.wait_ge(*act_rms.at(it, (s, 0)))
                    act.activation(RMSB[s], RMSB[s], ACT.Exp, scale=-0.5).then_inc(*act_rms.step((s, 1)))

                def y_hi(it, s):
                    for b in range(NB):
                        act.wait_ge(*pe_p1.at(it, (s, b)))
                        if b == 0:
                            act.wait_ge(*pool_deg.at(it, (s, 5), 1))
                        bank = work_bank(("p1", s, b))
                        act.activation(XH[s][:, b, :], bank[:, D:2 * D], ACT.Copy, scale=DRS[s][:, 1, b:b + 1])
                        act.activation(PA[s][:, b, :], bank[:, 0:D], ACT.Copy).then_inc(*act_p1.step((s, b)))

                def soft(it, s):
                    act.wait_ge(*dve_pre.at(it, (s, NB - 1)))
                    act.activation(TMP[s], PA[s], ACT.Abs).then_inc(*act_soft.step((s, 0)))
                    act.wait_ge(*act_soft.at(it, (s, 0)))
                    act.activation(TMP[s], TMP[s], ACT.Exp, scale=-1.0).then_inc(*act_soft.step((s, 1)))
                    act.wait_ge(*act_soft.at(it, (s, 1)))
                    act.activation(TMP[s], TMP[s], ACT.Ln, bias=1.0).then_inc(*act_soft.step((s, 2)))

                for s in SLOTS:
                    keep_adjT(0, s)
                    for w in range(2):
                        hi_part(0, s, 0, w)

                with act.Fori(1, PAIRS + 1) as it:
                    for i in range(STREAM):
                        if i < TILES:
                            act.wait_ge(*dve_max.at(it, i))
                            if i >= PROBS:
                                act.wait_ge(*pe_pT.at(it, i - PROBS))
                            act.activation(PR[:, i % PROBS, :], SM[:, i % MASKED, :], ACT.Exp, scale=-1.0,
                                           bias=NMAX[:, i % MASKED:i % MASKED + 1],
                                           accum_out=RS[:, i // SEG_TILES % 2, i % SEG_TILES:i % SEG_TILES + 1]
                                           ).then_inc(*act_exp.step(i))
                        t = i - LAG
                        if 0 <= t < TILES and t % 2:
                            act.wait_ge(*pe_pT.at(it, t))
                            _, _, b, j = tile_of(t)
                            act.activation(PT[:, t // 8 % 2, j, :, b % 2 * P:(b % 2 + 1) * P],
                                           work_bank(("pT", t))[:, :].rearrange("p (k q) -> p k q", q=P),
                                           ACT.Copy).then_inc(*act_pT.step(t))
                        if qk_at(i):
                            hi_part(it, *qk_at(i))
                        if (q := segment_at(i, 22)) is not None:
                            act.wait_ge(*pe_rb.at(it, q))
                            if q:
                                act.wait_ge(*dve_attn.at(it, q - 1))
                            act.activation(RBS[:, :], work_bank(("rb", q))[:, :], ACT.Copy).then_inc(*act_rb.step(q))

                    x_hi(it, 0, 0)
                    sums(it, 1, 0)
                    hidden(it, 1, 0, 0)
                    x_hi(it, 0, 1)
                    for k in range(1, HIDDEN[1]):
                        hidden(it, 1, 0, k)
                    sums(it, 1, 1)
                    hidden(it, 1, 1, 0)
                    hidden(it, 1, 1, 1)
                    x_hi(it, 1, 0)
                    hidden(it, 1, 1, 2)
                    hidden(it, 1, 1, 3)
                    sums(it, 2, 0)
                    x_hi(it, 1, 1)
                    sums(it, 2, 1)
                    inverse_rms(it, 0)
                    inverse_rms(it, 1)
                    for s in SLOTS:
                        for k in range(HIDDEN[2]):
                            hidden(it, 2, s, k)
                    y_hi(it, 0)
                    soft(it, 0)
                    y_hi(it, 1)
                    keep_adjT(it, 0)
                    for w in range(2):
                        hi_part(it, 0, 0, w)
                    soft(it, 1)
                    keep_adjT(it, 1)
                    for w in range(2):
                        hi_part(it, 1, 0, w)

            @block.vector
            def _(dve):
                def lo_part(it, s, g, w):
                    dve.wait_ge(*act_hi.at(it, (s, g, w)))
                    dve.scalar_tensor_tensor(out=STG[w][:, 1, :], in0=work_bank(("qk", s, g, w))[:, :],
                                             scalar=bqk[:, w, g:g + 1], in1=STG[w][:, 0, :],
                                             op0=ALU.add, op1=ALU.subtract).then_inc(*dve_lo.step((s, g, w)))

                def keep_xT(it, s):
                    for c in range(DC):
                        dve.wait_ge(*pe_xT.at(it, (s, c)))
                        dve.tensor_copy(XT[s][:, c, :], work_bank(("xT", s, c))[:, :]).then_inc(*dve_xT.step((s, c)))

                def degree_in(it, s):
                    dve.wait_ge(*adj_loaded[s].at(it, "adj"))
                    if type(it) is not int:
                        dve.wait_ge(*pool_deg.at(it, (s, 5), 1))
                    dve.tensor_reduce(DEG[s][:, 1, :], ADJ[s][:, :, :], AX.X, ALU.add).then_inc(*dve_din.step(s))

                def make_mask(it, s):
                    dve.wait_ge(*pe_adjT.at(it, (s, NB - 1)))
                    dve.wait_ge(*dve_din.at(it, s))
                    dve.tensor_scalar(ADJ[s][:, :, :], ADJ[s][:, :, :], 0.0, NEG, ALU.is_le, ALU.mult).then_inc(*dve_mask.step(s))

                def values(it, s):
                    for half in range(2):
                        dve.wait_ge(*pe_v.at(it, (s, half)))
                        if half == 0:
                            dve.wait_ge(*stored[s].at(it, "out"))
                        dve.tensor_tensor(VN[s][:, 2 * half:2 * half + 2, :],
                                          work_bank(("v", s, half))[:, :].rearrange("p (b d) -> p b d", d=D),
                                          bv_rows[:, :].unsqueeze(1).to_broadcast([P, 2, D]), ALU.add
                                          ).then_inc(*dve_v.step((s, half)))

                def norm_source(L, s):
                    return RES[s] if L < 3 else XN[s] if L == 3 else PA[s]

                def add_attention(it, s, half):
                    dve.wait_ge(*pool_res.at(it, (0, s), 1))
                    dve.wait_ge(*pe_wo.at(it, (s, half)))
                    rows = RES[s][:, 2 * half:2 * half + 2, :]
                    dve.tensor_tensor(rows, work_bank(("wo", s, half))[:, :].rearrange("p (b d) -> p b d", d=D), rows,
                                      ALU.add).then_inc(*dve_add.step((0, s, half)))

                def add_rows(it, L, s):
                    dve.wait_ge(*pool_res.at(it, (L, s)))
                    dve.wait_ge(*pe_used.at(it, (L, s, HIDDEN[L] - 1)))
                    for b in range(NB):
                        dve.tensor_tensor(RES[s][:, b, :], ACC[b][:, 0:D], RES[s][:, b, :],
                                          ALU.add).then_inc(*dve_add.step((L, s, b)))

                def statistics(it, L, s):
                    src = norm_source(L, s)
                    for b in range(NB):
                        if L < 3:
                            dve.wait_ge(*dve_add.at(it, (L, s, b // 2 if L == 0 else b)))
                        elif L == 3:
                            dve.wait_ge(*dve_norm.at(it, (2, s, b)))
                        elif b == 0:
                            dve.wait_ge(*dve_soft.at(it, (s, 1)))
                        dve.bn_stats(STATS[s][:, b, :], src[:, b, :]).then_inc(*dve_stat.step((L, s, b)))
                    for b in range(NB):
                        dve.compute_val(dve_stat.at(it, (L, s, b))[1])
                        dve.wait_ge(k_sem, 8)
                        dve.wait_ge(*dve_stat.at(it, (L, s, b)))
                        dve.bn_aggr(MV[s][:, b, :], STATS[s][:, b, :]).then_inc(*dve_aggr.step((L, s, b)))

                def normalise(it, L, s):
                    src, dst = norm_source(L, s), XN[s] if L < 3 else VN[s]
                    dve.wait_ge(*pool_rstd.at(it, (L, s)))
                    for b in range(NB):
                        dve.tensor_scalar(dst[:, b, :], src[:, b, :], MV[s][:, b, 0:1], RSTD[s][:, b:b + 1],
                                          ALU.subtract, ALU.mult).then_inc(*dve_norm.step((L, s, b)))

                def x_lo(it, L, s):
                    dve.wait_ge(*act_xh.at(it, (L, s)))
                    dve.tensor_tensor(XL[s], XN[s][:, :, :], XH[s], ALU.subtract).then_inc(*dve_xl.step((L, s)))

                def sums(it, L, s):
                    dve.wait_ge(*pe_agg.at(it, (L, s, 1)))
                    dve.tensor_copy(AG[s][:, 1, :], work_bank(("agg", L, s, 1))[:, :]).then_inc(*dve_agg.step((L, s)))

                def gram_terms(it, s):
                    for c in range(DC):
                        dve.wait_ge(*pe_gram.at(it, (s, c)))
                        dve.scalar_tensor_tensor(out=GV[s][:, c, :], in0=work_bank(("gram", s, c))[:, :],
                                                 scalar=gram_c[:, c:c + 1], in1=AG[s][:, c, :],
                                                 op0=ALU.add, op1=ALU.mult).then_inc(*dve_gram.step((s, c)))

                def scaled_hidden(it, s, k):
                    if k == 0:
                        dve.wait_ge(*act_rms.at(it, (s, 1)))
                    dve.wait_ge(*pe_hid.at(it, (2, s, k)))
                    n = hids.index((2, s, k)) - 2
                    if hids[n][0] == 2:
                        dve.wait_ge(*act_hid.at(it, hids[n]))
                    dve.scalar_tensor_tensor(out=ZB[k % 2], in0=work_bank(("hid", 2, s, k))[:, :],
                                             scalar=b_up[2][:, k:k + 1], in1=RMSB[s],
                                             op0=ALU.add, op1=ALU.mult).then_inc(*dve_z.step((s, k)))

                def keep_xnT(it, s):
                    for c in range(DC):
                        dve.wait_ge(*pe_xnT.at(it, (s, c)))
                        dve.tensor_scalar(XT[s][:, c, :], work_bank(("xnT", s, c))[:, :], gb[:, 0, c:c + 1],
                                          gb[:, 1, c:c + 1], ALU.mult, ALU.add).then_inc(*dve_xnT.step((s, c)))

                def y_lo(it, s, b):
                    dve.wait_ge(*act_p1.at(it, (s, b)))
                    dve.scalar_tensor_tensor(out=XL[s][:, b, :], in0=work_bank(("p1", s, b))[:, D:2 * D],
                                             scalar=DRS[s][:, 1, b:b + 1], in1=XH[s][:, b, :],
                                             op0=ALU.mult, op1=ALU.subtract).then_inc(*dve_yl.step((s, b)))

                def pre_activation(it, s):
                    dve.wait_ge(*pe_z.at(it, s))
                    for b in range(NB):
                        dve.scalar_tensor_tensor(out=PA[s][:, b, :], in0=ACC[b][:, 0:D], scalar=NSO[s][:, b:b + 1],
                                                 in1=PA[s][:, b, :], op0=ALU.mult, op1=ALU.add
                                                 ).then_inc(*dve_pre.step((s, b)))

                def residual(it, s):
                    dve.wait_ge(*act_soft.at(it, (s, 2)))
                    dve.scalar_tensor_tensor(out=PA[s], in0=PA[s], scalar=0.0, in1=TMP[s],
                                             op0=ALU.max, op1=ALU.add).then_inc(*dve_soft.step((s, 0)))
                    dve.wait_ge(*dve_soft.at(it, (s, 0)))
                    dve.tensor_tensor(PA[s], PA[s], XN[s][:, :, :], ALU.add).then_inc(*dve_soft.step((s, 1)))

                for s in SLOTS:
                    keep_xT(0, s)
                    degree_in(0, s)
                    make_mask(0, s)
                    for w in range(2):
                        lo_part(0, s, 0, w)
                    values(0, s)

                with dve.Fori(1, PAIRS + 1) as it:
                    for i in range(STREAM):
                        if i < TILES:
                            s, g, b, j = tile_of(i)
                            if i % SEG_TILES == 0:
                                dve.wait_ge(*dve_mask.at(it, s, 1))
                            if i >= MASKED:
                                dve.wait_ge(*act_exp.at(it, i - MASKED))
                            dve.compute_val(pe_scores.at(it, i)[1])
                            dve.wait_ge(k_sem, 8)
                            dve.wait_ge(*pe_scores.at(it, i))
                            dve.tensor_tensor_reduce(
                                SM[:, i % MASKED, :], banks[4 + i % SCORE_BANKS][:, :], ADJ[s][:, b, :], -float(HD) ** -0.5,
                                3.0e38, ALU.add, ALU.min, NMAX[:, i % MASKED:i % MASKED + 1]).then_inc(*dve_max.step(i))
                        t = i - LAG
                        if 0 <= t < TILES and t % 2 == 0:
                            dve.wait_ge(*pe_pT.at(it, t))
                            _, _, b, j = tile_of(t)
                            dve.tensor_copy(PT[:, t // 8 % 2, j, :, b % 2 * P:(b % 2 + 1) * P],
                                            work_bank(("pT", t))[:, :].rearrange("p (k q) -> p k q", q=P)
                                            ).then_inc(*dve_pT.step(t))
                        if qk_at(i):
                            lo_part(it, *qk_at(i))
                        if (q := segment_at(i, 18)) is not None:
                            dve.wait_ge(*act_exp.at(it, SEG_TILES * q + SEG_TILES - 1))
                            dve.reciprocal(RR[:, :], RS[:, q % 2, :]).then_inc(*dve_recip.step((q, 0)))
                            dve.wait_ge(*dve_recip.at(it, (q, 0)))
                            if q:
                                dve.wait_ge(*pe_rb.at(it, q - 1))
                            dve.tensor_copy(REXP[:, :].rearrange("p (t d) -> p t d", d=HD),
                                            RR[:, :].unsqueeze(2).to_broadcast([P, SEG_TILES, HD])
                                            ).then_inc(*dve_recip.step((q, 1)))
                        if (q := segment_at(i, 24)) is not None:
                            s, g = SEGMENTS[q]
                            dve.wait_ge(*act_rb.at(it, q))
                            dve.wait_ge(*pe_av.at(it, 2 * q + 1))
                            dve.tensor_tensor(AG[s][:, g, :], OUT_T[:, :], RBS[:, :], ALU.mult).then_inc(*dve_attn.step(q))
                        if i - 2 in WO_AT:
                            add_attention(it, 0, WO_AT.index(i - 2))
                        if i == TILES + 2:
                            statistics(it, 0, 0)
                        if i == TILES + 6:
                            normalise(it, 0, 0)

                    x_lo(it, 0, 0)
                    for half in range(2):
                        add_attention(it, 1, half)
                    statistics(it, 0, 1)
                    sums(it, 1, 0)
                    normalise(it, 0, 1)
                    x_lo(it, 0, 1)
                    sums(it, 1, 1)
                    add_rows(it, 1, 0)
                    statistics(it, 1, 0)
                    normalise(it, 1, 0)
                    x_lo(it, 1, 0)
                    add_rows(it, 1, 1)
                    statistics(it, 1, 1)
                    sums(it, 2, 0)
                    normalise(it, 1, 1)
                    gram_terms(it, 0)
                    x_lo(it, 1, 1)
                    sums(it, 2, 1)
                    gram_terms(it, 1)
                    for k in range(HIDDEN[2]):
                        scaled_hidden(it, 0, k)
                    for k in range(HIDDEN[2]):
                        scaled_hidden(it, 1, k)
                        if k == 1:
                            add_rows(it, 2, 0)
                            statistics(it, 2, 0)
                        if k == 2:
                            normalise(it, 2, 0)
                        if k == 3:
                            statistics(it, 3, 0)
                        if k == 4:
                            normalise(it, 3, 0)
                    keep_xnT(it, 0)
                    add_rows(it, 2, 1)
                    statistics(it, 2, 1)
                    y_lo(it, 0, 0)
                    y_lo(it, 0, 1)
                    normalise(it, 2, 1)
                    statistics(it, 3, 1)
                    y_lo(it, 0, 2)
                    y_lo(it, 0, 3)
                    normalise(it, 3, 1)
                    pre_activation(it, 0)
                    keep_xnT(it, 1)
                    y_lo(it, 1, 0)
                    y_lo(it, 1, 1)
                    residual(it, 0)
                    y_lo(it, 1, 2)
                    y_lo(it, 1, 3)
                    keep_xT(it, 0)
                    statistics(it, 4, 0)
                    degree_in(it, 0)
                    normalise(it, 4, 0)
                    pre_activation(it, 1)
                    make_mask(it, 0)
                    for w in range(2):
                        lo_part(it, 0, 0, w)
                    values(it, 0)
                    residual(it, 1)
                    keep_xT(it, 1)
                    statistics(it, 4, 1)
                    degree_in(it, 1)
                    normalise(it, 4, 1)
                    make_mask(it, 1)
                    for w in range(2):
                        lo_part(it, 1, 0, w)
                    values(it, 1)

            @block.gpsimd
            def _(pool):
                def bias(it, L, s):
                    if L == 0:
                        for c in range(DC):
                            pool.wait_ge(*pe_xT.at(it, (s, c)))
                        src = RES[s]
                    else:
                        pool.wait_ge(*dve_norm.at(it, (L - 1, s, NB - 1)))
                        src = XN[s]
                    pool.tensor_tensor(RES[s][:, :, :], src[:, :, :], b_rows[L][:, :].unsqueeze(1).to_broadcast([P, NB, D]),
                                       ALU.add).then_inc(*pool_res.step((L, s)))

                def rstd(it, L, s):
                    pool.compute_val(dve_aggr.at(it, (L, s, NB - 1))[1])
                    pool.wait_ge(i_sem, 4)
                    pool.wait_ge(*dve_aggr.at(it, (L, s, NB - 1)))
                    pool.tensor_scalar(VE[s][:, :], MV[s][:, :, 1], LN_EPS, None, ALU.add).then_inc(*pool_var.step((L, s)))
                    pool.wait_ge(*pool_var.at(it, (L, s)))
                    pool.tensor_tensor(RSTD[s][:, :], VE[s][:, :], neg_half[:, 0:NB], ALU.pow).then_inc(*pool_rstd.step((L, s)))

                def degrees(it, s):
                    pool.wait_ge(*dve_pre.at(it, (s, NB - 1)))
                    pool.wait_ge(*act_adjT.at(it, (s, NB - 1)))
                    pool.compute_val(dve_din.at(it, s)[1])
                    pool.wait_ge(i_sem, 4)
                    pool.wait_ge(*dve_din.at(it, s))
                    pool.tensor_scalar(DNZ[s][:, :, :], DEG[s][:, :, :], 0.0, None, ALU.is_equal).then_inc(*pool_deg.step((s, 0)))
                    pool.wait_ge(*pool_deg.at(it, (s, 0)))
                    pool.tensor_tensor(DSC[s][:, :, :], DEG[s][:, :, :], DNZ[s][:, :, :], ALU.add).then_inc(*pool_deg.step((s, 1)))
                    pool.compute_val(pool_deg.at(it, (s, 1))[1])
                    pool.wait_ge(i_sem, 4)
                    pool.wait_ge(*pool_deg.at(it, (s, 1)))
                    pool.tensor_scalar(DNZ[s][:, :, :], DNZ[s][:, :, :], -1.0, 1.0, ALU.mult, ALU.add).then_inc(*pool_deg.step((s, 2)))
                    pool.tensor_tensor(DSC[s][:, :, :], DSC[s][:, :, :], neg_half[:, :].rearrange("p (a b) -> p a b", a=2),
                                       ALU.pow).then_inc(*pool_deg.step((s, 3)))
                    pool.wait_ge(*pool_deg.at(it, (s, 3)))
                    pool.tensor_tensor(DRS[s][:, :, :], DSC[s][:, :, :], DNZ[s][:, :, :], ALU.mult).then_inc(*pool_deg.step((s, 4)))
                    pool.compute_val(pool_deg.at(it, (s, 4))[1])
                    pool.wait_ge(i_sem, 4)
                    pool.wait_ge(*pool_deg.at(it, (s, 4)))
                    pool.tensor_scalar(NSO[s][:, :], DRS[s][:, 0, :], -1.0, None, ALU.mult).then_inc(*pool_deg.step((s, 5)))

                for s in SLOTS:
                    bias(0, 0, s)
                    degrees(0, s)

                with pool.Fori(1, PAIRS + 1) as it:
                    rstd(it, 0, 0)
                    rstd(it, 0, 1)
                    bias(it, 1, 0)
                    bias(it, 1, 1)
                    rstd(it, 1, 0)
                    bias(it, 2, 0)
                    rstd(it, 1, 1)
                    bias(it, 2, 1)
                    rstd(it, 2, 0)
                    rstd(it, 3, 0)
                    rstd(it, 2, 1)
                    rstd(it, 3, 1)
                    bias(it, 0, 0)
                    rstd(it, 4, 0)
                    degrees(it, 0)
                    rstd(it, 4, 1)
                    bias(it, 0, 1)
                    degrees(it, 1)


_INS = ['x', 'adj', 'L0_gnn_Wq', 'L0_gnn_bq', 'L0_gnn_Wk', 'L0_gnn_bk', 'L0_gnn_Wv', 'L0_gnn_bv', 'L0_gnn_Wo',
        'L0_gnn_bo', 'L1_gnn_eps', 'L1_gnn_W1', 'L1_gnn_b1', 'L1_gnn_W2', 'L1_gnn_b2', 'L2_gnn_epsilon',
        'L2_gnn_W1', 'L2_gnn_b1', 'L2_gnn_rms_weight', 'L2_gnn_W2', 'L2_gnn_b2', 'L3_gnn_gamma', 'L3_gnn_beta',
        'L3_gnn_W_self', 'L3_gnn_W_neigh']


def kernel(**inputs):
    import numpy as _np
    import concourse.bacc as _bacc
    from concourse import mybir as _mybir
    from concourse.bass_utils import run_bass_kernel_spmd as _run

    nc = _bacc.Bacc("TRN2", target_bir_lowering=False, num_devices=1)
    arrays, args = {}, []
    for name in _INS:
        a = _np.ascontiguousarray(inputs[name])
        if a.ndim == 0:
            a = a.reshape(1)
        arrays[f"in_{name}"] = a
        args.append(nc.dram_tensor(f"in_{name}", a.shape, _mybir.dt.from_np(a.dtype), kind="ExternalInput").ap())
    args.append(nc.dram_tensor("out", (N_GRAPHS, N, D), F32, kind="ExternalOutput").ap())
    build(nc, *args)
    r = _run(nc, [arrays], core_ids=[0])
    return r.results[0]["out"]
```

```python
from contextlib import ExitStack

import concourse.bass as bass
from concourse import mybir

ALU = mybir.AluOpType
ACT = mybir.ActivationFunctionType
AX = mybir.AxisListType
F32 = mybir.dt.float32
F32R = mybir.dt.float32r
BF16 = mybir.dt.bfloat16

P = 128
N_GRAPHS, N, D = 32, 512, 256
NB = N // P
DC = D // P
HEADS, HD = 8, 32
GH = P // HD
H1, H2 = 512, 1024
HIDDEN = {1: H1 // P, 2: H2 // P}
PAIRS = N_GRAPHS // 2
NEG = -9000000000000000.0
SLOTS = (0, 1)
LN_EPS = 1e-5
RMS_EPS = 1e-6

SEGMENTS = [(s, g) for g in range(HEADS // GH) for s in SLOTS]
SEG_TILES = NB * GH
TILES = SEG_TILES * len(SEGMENTS)
LAG = 3
STREAM = TILES + 9
SCORE_BANKS, MASKED, PROBS = 3, 3, 4
PARTS = ((0, 0), (0, 1), (1, 0))
SET_TILES = 2 * GH
SETS = TILES // SET_TILES
BY_VECTOR = (1, 4, 7)
WO_AT = {55: (0, 0), 61: (0, 1)}


def tile_of(i):
    s, g = SEGMENTS[i // SEG_TILES]
    return s, g, i % SEG_TILES // GH, i % GH


def qk_at(i):
    return {9: (0, 1, 0), 17: (0, 1, 1), 25: (1, 1, 0), 33: (1, 1, 1)}.get(i)


def set_at(i, offset):
    p, r = divmod(i - offset, SET_TILES)
    return p if r == 0 and 0 <= p < SETS else None


def outputs_at(i):
    for p in range(SETS):
        if 0 <= (k := i - SET_TILES * p - (13 if p < SETS - 1 else 12)) < NB:
            return p, k
    return None


def attn_at(i):
    return SETS - 1 if i == STREAM - 1 else p if (p := set_at(i, 18)) != SETS - 1 else None


class Signal:

    def __init__(self, sem, keys, by=1, ahead=()):
        keys = [k for k in keys if k not in ahead] + list(ahead)
        self.credit = (len(keys) - len(ahead)) * by
        self.sem, self.by, self.total = sem, by, len(keys) * by
        self.place = {k: (n + 1) * by for n, k in enumerate(keys)}
        self.keys, self.next = list(keys), len(keys) - len(ahead)

    def step(self, key):
        assert self.keys[self.next % len(self.keys)] == key, (key, self.keys[self.next % len(self.keys)])
        self.next += 1
        return self.sem, self.by

    def at(self, it, key, turns_back=0):
        return self.sem, it * self.total + (self.place[key] - turns_back * self.total)


def build(nc, x, adj, Wq, bq, Wk, bk, Wv, bv, Wo, bo, eps1, W1, b1, W2, b2,
          eps2, V1, c1, rms_w, V2, c2, gamma, beta, W_self, W_neigh, out):
    ctx = ExitStack()
    with ctx:
        def sb(name, shape, dt=F32):
            return ctx.enter_context(nc.sbuf_tensor(name, shape, dt))

        ident = sb("ident", [P, P])
        ones = sb("ones", [P, P])
        neg_half = sb("neg_half", [P, 8])
        diag = {1: sb("diag1", [P, P]), 2: sb("diag2", [P, P])}
        wq, wk, wv, wo = (sb(n, [P, DC, D]) for n in ("wq", "wk", "wv", "wo"))
        w_up = {1: [sb(f"w1_{n}", [P, DC, H1], F32R) for n in ("hi", "lo")],
                2: [sb(f"v1_{n}", [P, DC, H2], F32R) for n in ("hi", "lo")]}
        w_down = {1: sb("w2", [P, HIDDEN[1], D]), 2: sb("v2", [P, HIDDEN[2], D])}
        w_cat = sb("w_cat", [P, DC, 2 * D])
        gram = [sb(f"gram_{n}", [P, DC, D], F32R) for n in ("hi", "lo")]
        bqk = sb("bqk", [P, 2, DC])
        b_up = {1: sb("b1c", [P, HIDDEN[1]]), 2: sb("c1c", [P, HIDDEN[2]])}
        rms = sb("rms", [P, HIDDEN[2]])
        gb = sb("gb", [P, 2, DC])
        bv_rows = sb("bv_rows", [P, D])
        b_rows = {0: sb("bo_rows", [P, D]), 1: sb("b2_rows", [P, D]), 2: sb("c2_rows", [P, D])}
        eps_col = sb("eps_col", [P, 2])
        gram_c = sb("gram_c", [P, DC])
        sq_eps = sb("sq_eps", [P, 1])
        small = sb("small", [P, 16])

        def two(name, shape, dt=F32):
            return [sb(f"{name}{s}", shape, dt) for s in SLOTS]

        RES = two("res", [P, NB, D])
        XN = two("xn", [P, NB, D])
        MASK = two("mask", [P, NB, N], BF16)
        ADJT = two("adjT", [P, NB, N], F32R)
        XT = two("xT", [P, DC, N])
        AG = two("ag", [P, DC, N])
        VN = two("vn", [P, NB, D])
        STK = two("stk", [P, 2, GH, N], F32R)
        PT = sb("pT", [P, 2, GH, NB, 2 * P])
        SM = sb("masked", [P, MASKED, N])
        PR = sb("probs", [P, PROBS, N])
        REXP = sb("rexp", [P, N])
        RBS = sb("rbs", [P, N])
        NMAX = sb("nmax", [P, MASKED])
        RS = sb("rs", [P, 2, SET_TILES])
        RR = sb("rr", [P, SET_TILES])
        STATS = two("stats", [P, NB, 6])
        MV = two("mv", [P, NB, 2])
        VE = two("ve", [P, NB])
        RSTD = two("rstd", [P, NB])
        DEG = two("deg", [P, 2, NB])
        DNZ = two("dnz", [P, 2, NB])
        DSC = two("dsc", [P, 2, NB])
        DRS = two("drs", [P, 2, NB])
        NSO = two("nso", [P, NB])
        ADJ = [PR[:, :, :], PT[:, 1, 2:4, :, :].rearrange("p j (a h) q -> p (j a) (h q)", h=2)]
        STG = [[b.rearrange("p (a h) q -> p a (h q)", h=2).bitcast(F32R) for b in bufs]
               for bufs in ([PT[:, 0, 2, :, :], PT[:, 0, 3, :, :]], [XN[0][:, :, :], XN[1][:, :, :]])]
        AGS = [[STK[s][:, 1, 2 * n:2 * n + 2, :] for n in range(2)] for s in SLOTS]
        XH = [STK[s][:, 0, 0:2, :].rearrange("p a (b d) -> p (a b) d", d=D) for s in SLOTS]
        XL = [STK[s][:, 0, 2:4, :].rearrange("p a (b d) -> p (a b) d", d=D) for s in SLOTS]
        HB = [PT[:, 0, n, 0:2, :].rearrange("p a b -> p (a b)") for n in range(3)]
        ZB = [PT[:, 0, n, 2:4, :].rearrange("p a b -> p (a b)") for n in range(2)]
        RMSB = [REXP[:, :], RBS[:, :]]
        PA = [AG[s][:, :, :].rearrange("p c (b d) -> p (c b) d", d=D) for s in SLOTS]
        TMP = [PT[:, 1, s, :, :] for s in SLOTS]
        GV = [VN[s][:, :, :].rearrange("p (c b) d -> p c (b d)", c=DC) for s in SLOTS]

        banks = [ctx.enter_context(nc.psum_tensor(f"bank{n}", [P, N], F32)) for n in range(8)]
        ACC = banks[4:8]
        OUT_T = banks[7]

        w_sem = ctx.enter_context(nc.semaphore("weights_loaded"))
        v_sem = ctx.enter_context(nc.semaphore("hidden_weights_loaded"))
        i_sem = ctx.enter_context(nc.semaphore("ident_ready"))
        t_sem = ctx.enter_context(nc.semaphore("v1T_in_psum"))
        u_sem = ctx.enter_context(nc.semaphore("v1T_copied"))
        g_sem = ctx.enter_context(nc.semaphore("gram_in_psum"))
        k_sem = ctx.enter_context(nc.semaphore("constants_done"))
        s_sem = ctx.enter_context(nc.semaphore("weights_split"))
        whole = PT[:, 1, :, :, :].rearrange("p a b c -> p (a b c)")
        WHOLE = {2: whole[:, 0:DC * H2].rearrange("p (c n) -> p c n", c=DC),
                 1: whole[:, DC * H2:DC * (H1 + H2)].rearrange("p (c n) -> p c n", c=DC)}
        V1T = PT[:, 0, :, :, :].rearrange("p a b c -> p (a b c)").rearrange("p (k d) -> p k d", d=D)[:, 0:HIDDEN[2], :]

        def rows_to_all(v):
            return v.rearrange("(a n) -> a n", a=1)[0:1, :].to_broadcast([P, v.shape[0]])

        signals = []

        def signal(name, keys, by=1, ahead=()):
            s = Signal(ctx.enter_context(nc.semaphore(name)), keys, by, ahead)
            signals.append(s)
            return s

        chunks = [(s, c) for s in SLOTS for c in range(DC)]
        blocks = [(s, b) for s in SLOTS for b in range(NB)]
        qk1, qk0 = ([(s, g, w) for s in SLOTS for w in range(2)] for g in (1, 0))
        hids = [(L, s, k) for L in (1, 2) for s in SLOTS for k in range(HIDDEN[L])]
        tiles = list(range(TILES))
        acc_blocks = [(0, s, h) for s in SLOTS for h in range(2)] + [(L, s, b) for L in (1, 2) for s, b in blocks]
        norms = [(0, 0), (0, 1), (1, 0), (1, 1), (2, 0), (3, 0), (2, 1), (3, 1), (4, 0), (4, 1)]
        norm_blocks = [(L, s, b) for L, s in norms for b in range(NB)]

        x_loaded = [signal(f"x_loaded{s}", [], 16, ahead=["x"]) for s in SLOTS]
        adj_loaded = [signal(f"adj_loaded{s}", [], 16, ahead=["adj"]) for s in SLOTS]
        spilled = [signal(f"spilled{w}", [(s, 1) for s in SLOTS], 16, ahead=[(s, 0) for s in SLOTS]) for w in range(2)]
        stacked = [[signal(f"stacked{s}{w}", [(1, r) for r in range(4)], 16, ahead=[(0, r) for r in range(4)])
                    for w in range(2)] for s in SLOTS]
        stored = [signal(f"stored{s}", ["out"], 16) for s in SLOTS]

        pe_xT = signal("pe_xT", [], ahead=chunks)
        pe_adjT = signal("pe_adjT", [], ahead=blocks)
        pe_qk = signal("pe_qk", qk1, ahead=qk0)
        v1, v0 = ([(s, h) for h in range(2)] for s in (1, 0))
        pe_v = signal("pe_v", v1, ahead=v0)
        pe_scores = signal("pe_scores", tiles)
        pe_pT = signal("pe_pT", tiles)
        pe_av = signal("pe_av", range(SETS))
        pe_rb = signal("pe_rb", range(SETS))
        pe_wo = signal("pe_wo", chunks)
        pe_agg = signal("pe_agg", [(L, s, c) for L in (1, 2) for s, c in chunks])
        pe_hid = signal("pe_hid", hids)
        pe_used = signal("pe_used", [h for h in hids if h[2] < HIDDEN[h[0]] - 1])
        pe_rows = signal("pe_rows", [(L, s, b) for L in (1, 2) for s, b in blocks])
        pe_gram = signal("pe_gram", chunks)
        pe_ms = signal("pe_ms", SLOTS)
        pe_xnT = signal("pe_xnT", chunks)
        pe_p1 = signal("pe_p1", blocks)
        pe_z = signal("pe_z", SLOTS)

        act_adjT = signal("act_adjT", [], ahead=blocks)
        act_hi = signal("act_hi", qk1, ahead=qk0)
        act_exp = signal("act_exp", tiles)
        act_pT = signal("act_pT", [i for i in tiles if i % SET_TILES not in BY_VECTOR])
        act_rb = signal("act_rb", range(SETS))
        act_xh = signal("act_xh", [(L, s) for L in range(2) for s in SLOTS])
        act_agg = signal("act_agg", [(L, s, c) for L in (1, 2) for s, c in chunks])
        act_hid = signal("act_hid", hids)
        act_rms = signal("act_rms", [(s, n) for s in SLOTS for n in range(2)])
        act_p1 = signal("act_p1", blocks)
        act_soft = signal("act_soft", [(s, n) for s in SLOTS for n in range(3)])

        dve_xT = signal("dve_xT", [], ahead=chunks)
        dve_din = signal("dve_din", [], ahead=SLOTS)
        dve_lo = signal("dve_lo", qk1, ahead=qk0)
        dve_mask = signal("dve_mask", [], ahead=SLOTS)
        dve_v = signal("dve_v", v1, ahead=v0)
        dve_max = signal("dve_max", tiles)
        dve_pT = signal("dve_pT", [i for i in tiles if i % SET_TILES in BY_VECTOR])
        dve_recip = signal("dve_recip", [(p, n) for p in range(SETS) for n in range(2)])
        dve_attn = signal("dve_attn", range(SETS))
        dve_add = signal("dve_add", acc_blocks)
        dve_stat = signal("dve_stat", norm_blocks)
        dve_aggr = signal("dve_aggr", norm_blocks)
        dve_norm = signal("dve_norm", [n for n in norm_blocks if n[0] < 4])
        dve_xl = signal("dve_xl", [(L, s) for L in range(2) for s in SLOTS])
        dve_agg = signal("dve_agg", [(L, s, c) for L in (1, 2) for s in SLOTS for c in range(DC + L - 1)])
        dve_gram = signal("dve_gram", chunks)
        dve_z = signal("dve_z", [(s, k) for s in SLOTS for k in range(HIDDEN[2])])
        dve_xnT = signal("dve_xnT", chunks)
        dve_yl = signal("dve_yl", blocks)
        dve_pre = signal("dve_pre", blocks)
        dve_soft = signal("dve_soft", [(0, 0), (1, 0), (1, 1)])

        pool_res = signal("pool_res", [(L, s) for L in (1, 2) for s in SLOTS], ahead=[(0, s) for s in SLOTS])
        pool_var = signal("pool_var", norms)
        pool_rstd = signal("pool_rstd", norms)
        pool_sum = signal("pool_sum", [0])
        pool_out = signal("pool_out", blocks)
        pool_deg = signal("pool_deg", [], ahead=[(s, n) for s in SLOTS for n in range(6)])

        def used(it, hid):
            L, s, k = hid
            return pe_rows.at(it, (L, s, NB - 1)) if k == HIDDEN[L] - 1 else pe_used.at(it, hid)

        work = []
        for i in range(STREAM):
            t = i - LAG
            if i < 2:
                work.append((("v", 1, i), dve_v, (1, i)))
            if 0 <= t < TILES:
                work.append((("pT", t), dve_pT if t % SET_TILES in BY_VECTOR else act_pT, t))
            if qk_at(i):
                work.append((("qk", *qk_at(i)), dve_lo, qk_at(i)))
            if (p := set_at(i, 14)) is not None:
                work.append((("rb", p), act_rb, p))
            if i in WO_AT:
                work.append((("wo", *WO_AT[i]), dve_add, (0, *WO_AT[i])))

        def work_agg(L, s):
            return [(("agg", L, s, c), dve_agg, (L, s, 2 if (L, c) == (2, 1) else c)) for c in range(DC)]

        def work_hid(L, s):
            return [(("hid", L, s, k), *((act_hid, (L, s, k)) if L == 1 else (dve_z, (s, k)))) for k in range(HIDDEN[L])]

        def work_gram(s):
            return [(("gram", s, c), dve_gram, (s, c)) for c in range(DC)]

        def work_ms(s):
            return [(("ms", s), act_rms, (s, 0))]

        def work_xnT(s):
            return [(("xnT", s, c), dve_xnT, (s, c)) for c in range(DC)]

        def work_p1(s):
            return [(("p1", s, b), dve_yl, (s, b)) for b in range(NB)]

        def work_xT(s):
            return [(("xT", s, c), dve_xT, (s, c)) for c in range(DC)]

        def work_adjT(s):
            return [(("adjT", s, b), act_adjT, (s, b)) for b in range(NB)]

        def work_wo(s, h):
            return [(("wo", s, h), dve_add, (0, s, h))]

        def work_qk(s):
            return [(("qk", s, 0, w), dve_lo, (s, 0, w)) for w in range(2)]

        work += work_wo(1, 0) + work_agg(1, 0) + work_wo(1, 1)
        work += work_hid(1, 0) + work_agg(1, 1) + work_hid(1, 1)
        work += work_agg(2, 0) + work_gram(0) + work_hid(2, 0)[:1] + work_ms(0) + work_agg(2, 1)
        work += work_gram(1) + work_ms(1) + work_hid(2, 0)[1:] + work_hid(2, 1)
        work += work_xnT(0) + work_p1(0) + work_xT(0) + work_xnT(1) + work_adjT(0) + work_p1(1) + work_qk(0)
        work += work_xT(1) + [(("v", 0, h), dve_v, (0, h)) for h in range(2)] + work_adjT(1) + work_qk(1)
        while len(work) % 4:
            work.append((None, None, None))
        place = {w[0]: n for n, w in enumerate(work)}

        def work_bank(key):
            return banks[place[key] % 4]

        def in_entry(key):
            return key[0] in ("xT", "adjT") or key[:2] == ("v", 0) or key[0] == "qk" and key[2] == 0

        def bank_read(it, key):
            n, back = place[key] - 4, 0
            if type(it) is int:
                entries = [m for m in range(n, -1, -4) if work[m][0] and in_entry(work[m][0])]
                n = entries[0] if entries else n
            while n < 0 or work[n][0] is None:
                if n < 0:
                    n, back = n + len(work), 1
                else:
                    n -= 4
            return work[n][1].at(it, work[n][2], back)

        x_v = x.rearrange("g (t p) d -> g p t d", p=P)
        adj_v = adj.rearrange("g (t p) m -> g p t m", p=P)
        out_v = out.rearrange("g (t p) d -> g p t d", p=P)
        scratch = [[nc.dram_tensor(f"qk_parts{s}{w}", (2, P, N), F32).ap() for w in range(2)] for s in SLOTS]

        with nc.Block() as setup:
            @setup.sync
            def _(sp):
                sp.dma_start(WHOLE[2], V1.rearrange("(c p) n -> p c n", p=P)).then_inc(v_sem, 16)
                sp.dma_start(b_up[2][:, :], c1.rearrange("(c p) -> p c", p=P), allow_slow_non_contiguous=True).then_inc(v_sem, 16)
                sp.dma_start(WHOLE[1], W1.rearrange("(c p) n -> p c n", p=P)).then_inc(w_sem, 16)
                for dst, src in ((wq, Wq), (wk, Wk), (wv, Wv), (wo, Wo)):
                    sp.dma_start(dst[:, :, :], src.rearrange("(c p) n -> p c n", p=P)).then_inc(w_sem, 16)
                for dst, src in ((w_down[1], W2), (w_down[2], V2)):
                    sp.dma_start(dst[:, :, :], src.rearrange("(c p) n -> p c n", p=P)).then_inc(w_sem, 16)
                for h, src in enumerate((W_self, W_neigh)):
                    sp.dma_start(w_cat[:, :, h * D:(h + 1) * D], src.rearrange("(c p) n -> p c n", p=P)).then_inc(w_sem, 16)
                for dst, src in ((bqk[:, 0, :], bq), (bqk[:, 1, :], bk), (b_up[1][:, :], b1), (rms[:, :], rms_w),
                                 (gb[:, 0, :], gamma), (gb[:, 1, :], beta)):
                    sp.dma_start(dst, src.rearrange("(c p) -> p c", p=P), allow_slow_non_contiguous=True).then_inc(w_sem, 16)
                for dst, src in ((bv_rows[:, :], bv), (b_rows[0][:, :], bo),
                                 (b_rows[1][:, :], b2), (b_rows[2][:, :], c2),
                                 (eps_col[:, 0:1], eps1), (eps_col[:, 1:2], eps2)):
                    sp.dma_start(dst, rows_to_all(src)).then_inc(w_sem, 16)
                sp.dma_start(RES[0][:, :, :], x_v[0]).then_inc(*x_loaded[0].step("x"))
                sp.dma_start(ADJ[0], adj_v[0]).then_inc(*adj_loaded[0].step("adj"))
                sp.dma_start(RES[1][:, :, :], x_v[1]).then_inc(*x_loaded[1].step("x"))
                sp.wait_ge(w_sem, 16 * 21)
                sp.wait_ge(v_sem, 32)

            @setup.gpsimd
            def _(pool):
                pool.memset(ident[:, :], 0.0).then_inc(i_sem, 1)
                pool.wait_ge(i_sem, 1)
                pool.affine_select(out=ident[:, :], in_=ident[:, :], compare_op=ALU.not_equal, fill=1.0,
                                   base=0, pattern=[[-1, P]], channel_multiplier=1).then_inc(i_sem, 1)
                pool.memset(ones[:, :], 1.0 / H2).then_inc(i_sem, 1)
                pool.memset(neg_half[:, :], -0.5).then_inc(i_sem, 1)
                pool.wait_ge(i_sem, 4)

            @setup.tensor
            def _(pe):
                pe.wait_ge(i_sem, 4)
                pe.wait_ge(v_sem, 32)
                for k in range(HIDDEN[2]):
                    for c in range(DC):
                        last = pe.transpose(banks[k // 2][:, (k % 2) * D + c * P:(k % 2) * D + (c + 1) * P],
                                            WHOLE[2][:, c, k * P:(k + 1) * P], ident[:, :])
                last.then_inc(t_sem, 1)
                pe.wait_ge(u_sem, 5)
                for c in range(DC):
                    for k in range(HIDDEN[2]):
                        pe.matmul(banks[4 + c][:, 0:D], V1T[:, k, c * P:(c + 1) * P], V1T[:, k, :],
                                  start=k == 0, stop=k == HIDDEN[2] - 1)
                    for k in range(HIDDEN[2]):
                        last = pe.matmul(banks[6 + c][:, 0:1], V1T[:, k, c * P:(c + 1) * P], b_up[2][:, k:k + 1],
                                         start=k == 0, stop=k == HIDDEN[2] - 1)
                last = pe.matmul(banks[0][:, 0:1], ones[:, :], small[:, 0:1], start=True, stop=True)
                last.then_inc(g_sem, 1)

            @setup.vector
            def _(dve):
                dve.wait_ge(t_sem, 1)
                for b in range(4):
                    dve.tensor_copy(V1T[:, 2 * b:2 * b + 2, :],
                                    banks[b][:, :].rearrange("p (k d) -> p k d", d=D)).then_inc(u_sem, 1)
                dve.tensor_tensor_reduce(small[:, 8:16], b_up[2][:, :], b_up[2][:, :], 1.0, 0.0, ALU.mult, ALU.add,
                                         small[:, 0:1]).then_inc(u_sem, 1)
                dve.wait_ge(w_sem, 16 * 21)
                for n, L in enumerate((2, 1)):
                    dve.tensor_copy(w_up[L][0][:, :, :], WHOLE[L]).then_inc(s_sem, 1)
                    dve.wait_ge(s_sem, 2 * n + 1)
                    dve.tensor_tensor(w_up[L][1][:, :, :], WHOLE[L], w_up[L][0][:, :, :], ALU.subtract).then_inc(s_sem, 1)
                dve.wait_ge(s_sem, 4)
                dve.tensor_tensor(w_cat[:, :, 0:D], w_cat[:, :, 0:D], w_cat[:, :, D:2 * D], ALU.add).then_inc(k_sem, 1)
                dve.scalar_tensor_tensor(out=diag[1][:, :], in0=ident[:, :], scalar=eps_col[:, 0:1], in1=ident[:, :],
                                         op0=ALU.mult, op1=ALU.add).then_inc(k_sem, 1)
                dve.tensor_scalar(diag[2][:, :], ident[:, :], eps_col[:, 1:2], None, ALU.mult).then_inc(k_sem, 1)
                dve.wait_ge(g_sem, 1)
                for c in range(DC):
                    dve.tensor_copy(gram[0][:, c, :], banks[4 + c][:, 0:D]).then_inc(k_sem, 1)
                    dve.wait_ge(k_sem, 4 + 3 * c)
                    dve.tensor_tensor(gram[1][:, c, :], banks[4 + c][:, 0:D], gram[0][:, c, :], ALU.subtract).then_inc(k_sem, 1)
                    dve.tensor_scalar(gram_c[:, c:c + 1], banks[6 + c][:, 0:1], 2.0, None, ALU.mult).then_inc(k_sem, 1)
                dve.tensor_scalar(sq_eps[:, :], banks[0][:, 0:1], RMS_EPS, None, ALU.add).then_inc(k_sem, 1)
                dve.wait_ge(k_sem, 10)

        with nc.Block() as block:
            @block.sync
            def _(sp):
                def stack(it, s, g):
                    for w in range(2):
                        if not (g == 0 and type(it) is int):
                            sp.compute_val(dve_lo.at(it, (s, g, w))[1])
                            sp.wait_ge(*stacked[s][w].at(it, (1 - g, 3), g))
                        sp.wait_ge(*dve_lo.at(it, (s, g, w)))
                        sp.dma_start(scratch[s][w].rearrange("a p n -> p a n"),
                                     STG[g][w].bitcast(F32)).then_inc(*spilled[w].step((s, g)))
                    if g:
                        sp.wait_ge(*pe_scores.at(it, SEG_TILES * SEGMENTS.index((s, 0)) + SEG_TILES - 1))
                    else:
                        sp.compute_val(spilled[0].at(it, (s, g))[1])
                        sp.wait_ge(*pe_z.at(it, s))
                    for w in range(2):
                        sp.wait_ge(*spilled[w].at(it, (s, g)))
                        for r in range(4):
                            part = r % 2 if w == 0 else r // 2
                            sp.dma_start(STK[s][r * HD:(r + 1) * HD, w, :, :].bitcast(F32),
                                         scratch[s][w][part].rearrange("(j p) n -> p j n", p=HD)
                                         ).then_inc(*stacked[s][w].step((g, r)))

                for s in signals:
                    if s.credit:
                        sp.sem_inc(s.sem, s.credit)
                sp.dma_start(ADJ[1], adj_v[1]).then_inc(*adj_loaded[1].step("adj"))
                for s in SLOTS:
                    stack(0, s, 0)
                with sp.Fori(1, PAIRS + 1) as it:
                    pair = sp.snap(it & (PAIRS - 1))
                    following = [sp.snap(pair * 2 + s) for s in SLOTS]
                    present = [sp.snap(it * 2 + (s - 2)) for s in SLOTS]
                    for s in SLOTS:
                        sp.compute_val(following[s])
                        sp.compute_val(present[s])
                    for s in SLOTS:
                        stack(it, s, 1)
                    for s in SLOTS:
                        used_by = pe_av.at(it, SETS - 1) if s else pe_pT.at(it, TILES - 1)
                        sp.compute_val(used_by[1])
                        sp.wait_ge(*used_by)
                        sp.dma_start(ADJ[s], adj_v[following[s]]).then_inc(*adj_loaded[s].step("adj"))
                    for s in SLOTS:
                        sp.wait_ge(*dve_norm.at(it, (2, s, NB - 1)))
                        sp.dma_start(RES[s][:, :, :], x_v[following[s]]).then_inc(*x_loaded[s].step("x"))
                    for s in SLOTS:
                        stack(it, s, 0)
                        sp.wait_ge(*pool_out.at(it, (s, NB - 1)))
                        sp.dma_start(out_v[present[s]], XN[s][:, :, :]).then_inc(*stored[s].step("out"))
                for s in SLOTS:
                    sp.wait_ge(stored[s].sem, stored[s].total * (PAIRS + 1))
                    sp.wait_ge(x_loaded[s].sem, x_loaded[s].total * (PAIRS + 1))
                    sp.wait_ge(adj_loaded[s].sem, adj_loaded[s].total * (PAIRS + 1))
                    for w in range(2):
                        sp.wait_ge(stacked[s][w].sem, stacked[s][w].total * (PAIRS + 1))
                for w in range(2):
                    sp.wait_ge(spilled[w].sem, spilled[w].total * (PAIRS + 1))

            @block.tensor
            def _(pe):
                def half_qk(it, s, g, w, c):
                    if c == 0:
                        pe.wait_ge(*bank_read(it, ("qk", s, g, w)))
                    last = pe.matmul(work_bank(("qk", s, g, w))[:, :], (wq, wk)[w][:, c, g * P:(g + 1) * P],
                                     XT[s][:, c, :], start=c == 0, stop=c == DC - 1)
                    if c == DC - 1:
                        last.then_inc(*pe_qk.step((s, g, w)))

                def transpose_x(it, s):
                    pe.wait_ge(*x_loaded[s].at(it, "x"))
                    for c in range(DC):
                        bank = work_bank(("xT", s, c))
                        pe.wait_ge(*bank_read(it, ("xT", s, c)))
                        for b in range(NB):
                            last = pe.transpose(bank[:, b * P:(b + 1) * P], RES[s][:, b, c * P:(c + 1) * P], ident[:, :])
                        last.then_inc(*pe_xT.step((s, c)))

                def transpose_adj(it, s):
                    pe.wait_ge(*adj_loaded[s].at(it, "adj"))
                    for m in range(NB):
                        bank = work_bank(("adjT", s, m))
                        pe.wait_ge(*bank_read(it, ("adjT", s, m)))
                        for b in range(NB):
                            last = pe.transpose(bank[:, b * P:(b + 1) * P], ADJ[s][:, b, m * P:(m + 1) * P], ident[:, :])
                        last.then_inc(*pe_adjT.step((s, m)))

                def first_qk(it, s):
                    pe.wait_ge(*dve_xT.at(it, (s, DC - 1)))
                    for w in range(2):
                        for c in range(DC):
                            half_qk(it, s, 0, w, c)

                def project_v(it, s, half):
                    bank = work_bank(("v", s, half))
                    pe.wait_ge(*bank_read(it, ("v", s, half)))
                    for b in range(2):
                        for c in range(DC):
                            nb = 2 * half + b
                            last = pe.matmul(bank[:, b * D:(b + 1) * D], XT[s][:, c, nb * P:(nb + 1) * P],
                                             wv[:, c, :], start=c == 0, stop=c == DC - 1)
                    last.then_inc(*pe_v.step((s, half)))

                def project_out(it, s, half):
                    bank = work_bank(("wo", s, half))
                    pe.wait_ge(*bank_read(it, ("wo", s, half)))
                    pe.wait_ge(*dve_attn.at(it, SETS // 2 + 2 * s + half))
                    for b in range(2):
                        nb = 2 * half + b
                        for c in range(DC):
                            last = pe.matmul(bank[:, b * D:(b + 1) * D], AG[s][:, c, nb * P:(nb + 1) * P], wo[:, c, :],
                                             start=c == 0, stop=c == DC - 1)
                    last.then_inc(*pe_wo.step((s, half)))

                def neighbour_sums(it, L, s, c):
                    pe.wait_ge(*act_adjT.at(it, (s, NB - 1), 1))
                    pe.wait_ge(*dve_xl.at(it, (L - 1, s)))
                    bank = work_bank(("agg", L, s, c))
                    pe.wait_ge(*bank_read(it, ("agg", L, s, c)))
                    for m in range(NB):
                        for n, part in enumerate((XH, XL)):
                            pe.matmul(bank[:, :], part[s][:, m, c * P:(c + 1) * P], ADJT[s][:, m, :],
                                      start=m == 0 and n == 0, stop=False)
                    for m in range(NB):
                        last = pe.matmul(bank[:, m * P:(m + 1) * P], XN[s][:, m, c * P:(c + 1) * P], diag[L][:, :],
                                         start=False, stop=m == NB - 1)
                    last.then_inc(*pe_agg.step((L, s, c)))

                def up(it, L, s, k):
                    if k == 0:
                        pe.wait_ge(*dve_agg.at(it, (L, s, 1)))
                    bank = work_bank(("hid", L, s, k))
                    pe.wait_ge(*bank_read(it, ("hid", L, s, k)))
                    for c in range(DC):
                        for n, (w, a) in enumerate(PARTS):
                            last = pe.matmul(bank[:, :], w_up[L][w][:, c, k * P:(k + 1) * P], AGS[s][a][:, c, :],
                                             start=c == 0 and n == 0, stop=c == DC - 1 and n == 2)
                    last.then_inc(*pe_hid.step((L, s, k)))

                def down(it, L, s, k):
                    if k == 0:
                        if (L, s) == (1, 0):
                            pe.wait_ge(*dve_max.at(it, TILES - 1))
                            pe.wait_ge(*dve_attn.at(it, SETS - 1))
                        else:
                            pe.wait_ge(*dve_add.at(it, (L, 0, NB - 1) if s else (L - 1, 1, NB - 1)))
                    pe.wait_ge(*act_hid.at(it, (L, s, k)))
                    slot = hids.index((L, s, k)) % 3
                    for b in range(NB):
                        last = pe.matmul(ACC[b][:, 0:D], HB[slot][:, b * P:(b + 1) * P], w_down[L][:, k, :],
                                         start=k == 0, stop=k == HIDDEN[L] - 1)
                        if k == HIDDEN[L] - 1:
                            last.then_inc(*pe_rows.step((L, s, b)))
                    if k < HIDDEN[L] - 1:
                        last.then_inc(*pe_used.step((L, s, k)))

                def gram_product(it, s):
                    for e in range(DC):
                        pe.wait_ge(*dve_agg.at(it, (2, s, e)))
                        for c in range(DC):
                            bank = work_bank(("gram", s, c))
                            if e == 0:
                                pe.wait_ge(*bank_read(it, ("gram", s, c)))
                            for n, (w, a) in enumerate(PARTS):
                                last = pe.matmul(bank[:, :], gram[w][:, e, c * P:(c + 1) * P], AGS[s][a][:, e, :],
                                                 start=e == 0 and n == 0, stop=e == DC - 1 and n == 2)
                            if e == DC - 1:
                                last.then_inc(*pe_gram.step((s, c)))

                def mean_square(it, s):
                    bank = work_bank(("ms", s))
                    pe.wait_ge(*bank_read(it, ("ms", s)))
                    for c in range(DC):
                        pe.wait_ge(*dve_gram.at(it, (s, c)))
                        last = pe.matmul(bank[:, :], ones[:, :], GV[s][:, c, :], start=c == 0, stop=c == DC - 1)
                    last.then_inc(*pe_ms.step(s))

                def transpose_xn(it, s):
                    pe.wait_ge(*dve_norm.at(it, (3, s, NB - 1)))
                    for c in range(DC):
                        bank = work_bank(("xnT", s, c))
                        pe.wait_ge(*bank_read(it, ("xnT", s, c)))
                        for b in range(NB):
                            last = pe.transpose(bank[:, b * P:(b + 1) * P], VN[s][:, b, c * P:(c + 1) * P], ident[:, :])
                        last.then_inc(*pe_xnT.step((s, c)))

                def both_weights(it, s):
                    for b in range(NB):
                        bank = work_bank(("p1", s, b))
                        pe.wait_ge(*bank_read(it, ("p1", s, b)))
                        pe.wait_ge(*dve_xnT.at(it, (s, DC - 1)))
                        for c in range(DC):
                            last = pe.matmul(bank[:, :], XT[s][:, c, b * P:(b + 1) * P], w_cat[:, c, :],
                                             start=c == 0, stop=c == DC - 1)
                        last.then_inc(*pe_p1.step((s, b)))

                def adj_y(it, s):
                    pe.wait_ge(*(dve_pre.at(it, (0, NB - 1)) if s else dve_add.at(it, (2, 1, NB - 1))))
                    for m in range(NB):
                        pe.wait_ge(*dve_yl.at(it, (s, m)))
                        for b in range(NB):
                            for n, part in enumerate((XH, XL)):
                                last = pe.matmul(ACC[b][:, 0:D], ADJT[s][:, m, b * P:(b + 1) * P], part[s][:, m, :],
                                                 start=m == 0 and n == 0, stop=m == NB - 1 and n == 1)
                    last.then_inc(*pe_z.step(s))

                transpose_x(0, 0)
                transpose_adj(0, 0)
                first_qk(0, 0)
                transpose_x(0, 1)
                for half in range(2):
                    project_v(0, 0, half)
                transpose_adj(0, 1)
                first_qk(0, 1)

                with pe.Fori(1, PAIRS + 1) as it:
                    for i in range(STREAM):
                        if i < TILES:
                            s, g, b, j = tile_of(i)
                            if i % SEG_TILES == 0:
                                for w in range(2):
                                    pe.wait_ge(*stacked[s][w].at(it, (g, 3), 1 - g))
                            if i < SCORE_BANKS:
                                pe.wait_ge(*dve_pre.at(it, (1, NB - 1), 1))
                            else:
                                pe.wait_ge(*dve_max.at(it, i - SCORE_BANKS))
                            pe.matmul(banks[4 + i % SCORE_BANKS][:, :], STK[s][:, 0, j, b * P:(b + 1) * P],
                                      STK[s][:, 1, j, :], start=True, stop=True).then_inc(*pe_scores.step(i))
                        if i < 2:
                            project_v(it, 1, i)
                        t = i - LAG
                        if 0 <= t < TILES:
                            bank = work_bank(("pT", t))
                            pe.wait_ge(*bank_read(it, ("pT", t)))
                            pe.wait_ge(*act_exp.at(it, t))
                            for k in range(NB):
                                last = pe.transpose(bank[:, k * P:(k + 1) * P], PR[:, t % PROBS, k * P:(k + 1) * P], ident[:, :])
                            last.then_inc(*pe_pT.step(t))
                        for c in range(DC):
                            if qk_at(i - c):
                                half_qk(it, *qk_at(i - c), c)
                        if (p := set_at(i, 14)) is not None:
                            bank = work_bank(("rb", p))
                            pe.wait_ge(*bank_read(it, ("rb", p)))
                            pe.wait_ge(*dve_recip.at(it, (p, 1)))
                            for b in range(2):
                                cols = slice((p % 2 * 2 + b) * P, (p % 2 * 2 + b + 1) * P)
                                last = pe.transpose(bank[:, cols], REXP[:, cols], ident[:, :])
                            last.then_inc(*pe_rb.step(p))
                        if outputs_at(i):
                            p, k = outputs_at(i)
                            s, g, b, _ = tile_of(SET_TILES * p)
                            if k == 0:
                                for signal_pT, by_vector in ((act_pT, False), (dve_pT, True)):
                                    pe.wait_ge(*signal_pT.at(it, max(
                                        t for t in range(SET_TILES * p, SET_TILES * (p + 1))
                                        if (t % SET_TILES in BY_VECTOR) == by_vector)))
                                pe.wait_ge(*dve_v.at(it, (s, 1), 1 - s))
                                if p == 0:
                                    pe.wait_ge(*dve_pre.at(it, (1, NB - 1), 1))
                                else:
                                    pe.wait_ge(*dve_attn.at(it, p - 1))
                            for j in range(GH):
                                h = g * GH + j
                                last = pe.matmul(OUT_T[j * HD:(j + 1) * HD, b * P:(b + 2) * P],
                                                 VN[s][:, k, h * HD:(h + 1) * HD], PT[:, p % 2, j, k, :],
                                                 start=k == 0, stop=k == NB - 1)
                            if k == NB - 1:
                                last.then_inc(*pe_av.step(p))
                        if i in WO_AT:
                            project_out(it, *WO_AT[i])

                    project_out(it, 1, 0)
                    for c in range(DC):
                        neighbour_sums(it, 1, 0, c)
                    project_out(it, 1, 1)
                    for s in SLOTS:
                        for k in range(HIDDEN[1] + 2):
                            if k == HIDDEN[1] and s == 0:
                                for c in range(DC):
                                    neighbour_sums(it, 1, 1, c)
                            if k < HIDDEN[1]:
                                up(it, 1, s, k)
                            if k >= 2:
                                down(it, 1, s, k - 2)
                    for c in range(DC):
                        neighbour_sums(it, 2, 0, c)
                    gram_product(it, 0)
                    up(it, 2, 0, 0)
                    mean_square(it, 0)
                    for c in range(DC):
                        neighbour_sums(it, 2, 1, c)
                    gram_product(it, 1)
                    mean_square(it, 1)
                    for s in SLOTS:
                        for k in range(HIDDEN[2] + 2):
                            if k == HIDDEN[2] and s == 1:
                                transpose_xn(it, 0)
                            if k < HIDDEN[2] and (s, k) != (0, 0):
                                up(it, 2, s, k)
                            if k >= 2:
                                down(it, 2, s, k - 2)

                    both_weights(it, 0)
                    transpose_x(it, 0)
                    adj_y(it, 0)
                    transpose_xn(it, 1)
                    transpose_adj(it, 0)
                    both_weights(it, 1)
                    first_qk(it, 0)
                    adj_y(it, 1)
                    transpose_x(it, 1)
                    for half in range(2):
                        project_v(it, 0, half)
                    transpose_adj(it, 1)
                    first_qk(it, 1)

            @block.scalar
            def _(act):
                def hi_part(it, s, g, w):
                    if s:
                        act.wait_ge(*spilled[w].at(it, (0, g)))
                    elif g:
                        act.wait_ge(*stored[w].at(it, "out", 1))
                    act.wait_ge(*pe_qk.at(it, (s, g, w)))
                    act.activation(STG[g][w][:, 0, :], work_bank(("qk", s, g, w))[:, :], ACT.Identity,
                                   bias=bqk[:, w, g:g + 1]).then_inc(*act_hi.step((s, g, w)))

                def keep_adjT(it, s, blocks_m=range(NB)):
                    for m in blocks_m:
                        if m == 0:
                            act.wait_ge(*pe_z.at(it, s))
                            if type(it) is not int:
                                act.wait_ge(*pool_deg.at(it, (s, 5), 1))
                        act.wait_ge(*pe_adjT.at(it, (s, m)))
                        act.activation(ADJT[s][:, m, :], work_bank(("adjT", s, m))[:, :], ACT.Copy,
                                       accum_out=DEG[s][:, 0, m:m + 1]).then_inc(*act_adjT.step((s, m)))

                def x_hi(it, L, s):
                    act.wait_ge(*dve_norm.at(it, (L, s, NB - 1)))
                    act.activation(XH[s], XN[s][:, :, :], ACT.Copy).then_inc(*act_xh.step((L, s)))

                def sums(it, L, s, c):
                    act.wait_ge(*pe_agg.at(it, (L, s, c)))
                    bank = work_bank(("agg", L, s, c))
                    if (L, c) == (2, 0):
                        act.activation(AG[s][:, c, :], bank[:, :], ACT.Copy)
                    act.activation(AGS[s][0][:, c, :], bank[:, :], ACT.Copy).then_inc(*act_agg.step((L, s, c)))

                def hidden(it, L, s, k):
                    n = hids.index((L, s, k))
                    if n >= 3:
                        act.wait_ge(*used(it, hids[n - 3]))
                    if L == 1:
                        act.wait_ge(*pe_hid.at(it, (1, s, k)))
                        act.activation(HB[n % 3], work_bank(("hid", 1, s, k))[:, :], ACT.Relu,
                                       bias=b_up[1][:, k:k + 1]).then_inc(*act_hid.step((1, s, k)))
                    else:
                        act.wait_ge(*dve_z.at(it, (s, k)))
                        act.activation(HB[n % 3], ZB[k % 2], ACT.Silu,
                                       scale=rms[:, k:k + 1]).then_inc(*act_hid.step((2, s, k)))

                def inverse_rms(it, s):
                    act.wait_ge(*pe_ms.at(it, s))
                    act.activation(RMSB[s], work_bank(("ms", s))[:, :], ACT.Ln, bias=sq_eps[:, :]).then_inc(*act_rms.step((s, 0)))
                    act.wait_ge(*act_rms.at(it, (s, 0)))
                    act.activation(RMSB[s], RMSB[s], ACT.Exp, scale=-0.5).then_inc(*act_rms.step((s, 1)))

                def y_hi(it, s):
                    for b in range(NB):
                        act.wait_ge(*pe_p1.at(it, (s, b)))
                        if b == 0:
                            act.wait_ge(*pool_deg.at(it, (s, 5), 1))
                        bank = work_bank(("p1", s, b))
                        act.activation(XH[s][:, b, :], bank[:, D:2 * D], ACT.Copy, scale=DRS[s][:, 1, b:b + 1])
                        act.activation(PA[s][:, b, :], bank[:, 0:D], ACT.Copy).then_inc(*act_p1.step((s, b)))

                def soft_exp(it, s):
                    act.wait_ge(*dve_pre.at(it, (s, NB - 1)))
                    act.activation(TMP[s], PA[s], ACT.Abs).then_inc(*act_soft.step((s, 0)))
                    act.wait_ge(*act_soft.at(it, (s, 0)))
                    act.activation(TMP[s], TMP[s], ACT.Exp, scale=-1.0).then_inc(*act_soft.step((s, 1)))

                def soft_log(it, s):
                    act.wait_ge(*act_soft.at(it, (s, 1)))
                    act.activation(TMP[s], TMP[s], ACT.Ln, bias=1.0).then_inc(*act_soft.step((s, 2)))

                for s in SLOTS:
                    keep_adjT(0, s)
                    for w in range(2):
                        hi_part(0, s, 0, w)

                with act.Fori(1, PAIRS + 1) as it:
                    for i in range(STREAM):
                        if qk_at(i - 1):
                            hi_part(it, *qk_at(i - 1))
                        if i < TILES:
                            act.wait_ge(*dve_max.at(it, i))
                            if i >= PROBS:
                                act.wait_ge(*pe_pT.at(it, i - PROBS))
                            act.activation(PR[:, i % PROBS, :], SM[:, i % MASKED, :], ACT.Exp, scale=-1.0,
                                           bias=NMAX[:, i % MASKED:i % MASKED + 1],
                                           accum_out=RS[:, i // SET_TILES % 2, i % SET_TILES:i % SET_TILES + 1]
                                           ).then_inc(*act_exp.step(i))
                        t = i - LAG
                        if 0 <= t < TILES and t % SET_TILES not in BY_VECTOR:
                            act.wait_ge(*pe_pT.at(it, t))
                            _, _, b, j = tile_of(t)
                            if t < SET_TILES and j >= 2:
                                act.wait_ge(*spilled[j - 2].at(it, (1, 0), 1))
                            act.activation(PT[:, t // SET_TILES % 2, j, :, b % 2 * P:(b % 2 + 1) * P],
                                           work_bank(("pT", t))[:, :].rearrange("p (k q) -> p k q", q=P),
                                           ACT.Copy).then_inc(*act_pT.step(t))
                        if (p := set_at(i, 15)) is not None:
                            cols = slice(p % 2 * D, (p % 2 + 1) * D)
                            act.wait_ge(*pe_rb.at(it, p))
                            if p >= 2:
                                act.wait_ge(*dve_attn.at(it, p - 2))
                            act.activation(RBS[:, cols], work_bank(("rb", p))[:, cols], ACT.Copy).then_inc(*act_rb.step(p))
                        if i == TILES + 3:
                            x_hi(it, 0, 0)

                    for c in range(DC):
                        sums(it, 1, 0, c)
                    hidden(it, 1, 0, 0)
                    x_hi(it, 0, 1)
                    for k in range(1, HIDDEN[1]):
                        hidden(it, 1, 0, k)
                    for c in range(DC):
                        sums(it, 1, 1, c)
                    hidden(it, 1, 1, 0)
                    hidden(it, 1, 1, 1)
                    x_hi(it, 1, 0)
                    hidden(it, 1, 1, 2)
                    hidden(it, 1, 1, 3)
                    for c in range(DC):
                        sums(it, 2, 0, c)
                    x_hi(it, 1, 1)
                    inverse_rms(it, 0)
                    for c in range(DC):
                        sums(it, 2, 1, c)
                    hidden(it, 2, 0, 0)
                    inverse_rms(it, 1)
                    for k in range(1, HIDDEN[2]):
                        hidden(it, 2, 0, k)
                    for k in range(HIDDEN[2]):
                        hidden(it, 2, 1, k)
                    y_hi(it, 0)
                    keep_adjT(it, 0)
                    soft_exp(it, 0)
                    y_hi(it, 1)
                    soft_log(it, 0)
                    for w in range(2):
                        hi_part(it, 0, 0, w)
                    soft_exp(it, 1)
                    keep_adjT(it, 1, range(2))
                    soft_log(it, 1)
                    hi_part(it, 1, 0, 0)
                    keep_adjT(it, 1, range(2, NB))
                    hi_part(it, 1, 0, 1)

            @block.vector
            def _(dve):
                def lo_part(it, s, g, w):
                    dve.wait_ge(*act_hi.at(it, (s, g, w)))
                    dve.scalar_tensor_tensor(out=STG[g][w][:, 1, :], in0=work_bank(("qk", s, g, w))[:, :],
                                             scalar=bqk[:, w, g:g + 1], in1=STG[g][w][:, 0, :],
                                             op0=ALU.add, op1=ALU.subtract).then_inc(*dve_lo.step((s, g, w)))

                def keep_xT(it, s):
                    for c in range(DC):
                        dve.wait_ge(*pe_xT.at(it, (s, c)))
                        dve.tensor_copy(XT[s][:, c, :], work_bank(("xT", s, c))[:, :]).then_inc(*dve_xT.step((s, c)))

                def degree_in(it, s):
                    dve.wait_ge(*adj_loaded[s].at(it, "adj"))
                    if type(it) is not int:
                        dve.wait_ge(*pool_deg.at(it, (s, 5), 1))
                    dve.tensor_reduce(DEG[s][:, 1, :], ADJ[s], AX.X, ALU.add).then_inc(*dve_din.step(s))

                def make_mask(it, s):
                    dve.wait_ge(*pe_adjT.at(it, (s, NB - 1)))
                    dve.wait_ge(*dve_din.at(it, s))
                    dve.tensor_scalar(MASK[s][:, :, :], ADJ[s], 0.0, NEG, ALU.is_le, ALU.mult).then_inc(*dve_mask.step(s))

                def values(it, s, half):
                    dve.wait_ge(*pe_v.at(it, (s, half)))
                    dve.tensor_tensor(VN[s][:, 2 * half:2 * half + 2, :],
                                      work_bank(("v", s, half))[:, :].rearrange("p (b d) -> p b d", d=D),
                                      bv_rows[:, :].unsqueeze(1).to_broadcast([P, 2, D]), ALU.add
                                      ).then_inc(*dve_v.step((s, half)))

                def norm_source(L, s):
                    return RES[s] if L < 3 else XN[s] if L == 3 else PA[s]

                def add_attention(it, s, half):
                    dve.wait_ge(*pool_res.at(it, (0, s), 1))
                    dve.wait_ge(*pe_wo.at(it, (s, half)))
                    rows = RES[s][:, 2 * half:2 * half + 2, :]
                    dve.tensor_tensor(rows, work_bank(("wo", s, half))[:, :].rearrange("p (b d) -> p b d", d=D), rows,
                                      ALU.add).then_inc(*dve_add.step((0, s, half)))

                def add_rows(it, L, s):
                    dve.wait_ge(*pool_res.at(it, (L, s)))
                    for b in range(NB):
                        dve.wait_ge(*pe_rows.at(it, (L, s, b)))
                        dve.tensor_tensor(RES[s][:, b, :], ACC[b][:, 0:D], RES[s][:, b, :],
                                          ALU.add).then_inc(*dve_add.step((L, s, b)))

                def statistics(it, L, s):
                    src = norm_source(L, s)
                    for b in range(NB):
                        if L < 3:
                            dve.wait_ge(*dve_add.at(it, (L, s, b // 2 if L == 0 else b)))
                        elif L == 3:
                            dve.wait_ge(*dve_norm.at(it, (2, s, b)))
                        elif b == 0:
                            dve.wait_ge(*(dve_soft.at(it, (1, 1)) if s else pool_sum.at(it, 0)))
                        dve.bn_stats(STATS[s][:, b, :], src[:, b, :]).then_inc(*dve_stat.step((L, s, b)))
                    for b in range(NB):
                        dve.compute_val(dve_stat.at(it, (L, s, b))[1])
                        dve.wait_ge(k_sem, 10)
                        dve.wait_ge(*dve_stat.at(it, (L, s, b)))
                        dve.bn_aggr(MV[s][:, b, :], STATS[s][:, b, :]).then_inc(*dve_aggr.step((L, s, b)))

                def normalise(it, L, s):
                    src, dst = norm_source(L, s), VN[s] if L == 3 else XN[s]
                    dve.wait_ge(*pool_rstd.at(it, (L, s)))
                    if L == 0:
                        dve.wait_ge(*stored[s].at(it, "out", 1))
                        dve.wait_ge(*spilled[s].at(it, (1, 1)))
                    for b in range(NB):
                        dve.tensor_scalar(dst[:, b, :], src[:, b, :], MV[s][:, b, 0:1], RSTD[s][:, b:b + 1],
                                          ALU.subtract, ALU.mult).then_inc(*dve_norm.step((L, s, b)))

                def x_lo(it, L, s):
                    dve.wait_ge(*act_xh.at(it, (L, s)))
                    dve.tensor_tensor(XL[s], XN[s][:, :, :], XH[s], ALU.subtract).then_inc(*dve_xl.step((L, s)))

                def sums(it, L, s, c):
                    dve.wait_ge(*act_agg.at(it, (L, s, c)))
                    bank = work_bank(("agg", L, s, c))
                    dve.tensor_tensor(AGS[s][1][:, c, :], bank[:, :], AGS[s][0][:, c, :],
                                      ALU.subtract).then_inc(*dve_agg.step((L, s, c)))
                    if (L, c) == (2, 1):
                        dve.tensor_copy(AG[s][:, 1, :], bank[:, :]).then_inc(*dve_agg.step((L, s, 2)))

                def gram_terms(it, s):
                    for c in range(DC):
                        if c == 0:
                            dve.wait_ge(*act_agg.at(it, (2, s, 0)))
                        else:
                            dve.wait_ge(*dve_agg.at(it, (2, s, 2)))
                        dve.wait_ge(*pe_gram.at(it, (s, c)))
                        dve.scalar_tensor_tensor(out=GV[s][:, c, :], in0=work_bank(("gram", s, c))[:, :],
                                                 scalar=gram_c[:, c:c + 1], in1=AG[s][:, c, :],
                                                 op0=ALU.add, op1=ALU.mult).then_inc(*dve_gram.step((s, c)))

                def scaled_hidden(it, s, k):
                    if k == 0:
                        dve.wait_ge(*act_rms.at(it, (s, 1)))
                    dve.wait_ge(*pe_hid.at(it, (2, s, k)))
                    n = hids.index((2, s, k)) - 2
                    if hids[n][0] == 2:
                        dve.wait_ge(*act_hid.at(it, hids[n]))
                    dve.scalar_tensor_tensor(out=ZB[k % 2], in0=work_bank(("hid", 2, s, k))[:, :],
                                             scalar=b_up[2][:, k:k + 1], in1=RMSB[s],
                                             op0=ALU.add, op1=ALU.mult).then_inc(*dve_z.step((s, k)))

                def keep_xnT(it, s):
                    for c in range(DC):
                        dve.wait_ge(*pe_xnT.at(it, (s, c)))
                        dve.tensor_scalar(XT[s][:, c, :], work_bank(("xnT", s, c))[:, :], gb[:, 0, c:c + 1],
                                          gb[:, 1, c:c + 1], ALU.mult, ALU.add).then_inc(*dve_xnT.step((s, c)))

                def y_lo(it, s, b):
                    dve.wait_ge(*act_p1.at(it, (s, b)))
                    dve.scalar_tensor_tensor(out=XL[s][:, b, :], in0=work_bank(("p1", s, b))[:, D:2 * D],
                                             scalar=DRS[s][:, 1, b:b + 1], in1=XH[s][:, b, :],
                                             op0=ALU.mult, op1=ALU.subtract).then_inc(*dve_yl.step((s, b)))

                def pre_activation(it, s):
                    dve.wait_ge(*pe_z.at(it, s))
                    for b in range(NB):
                        dve.scalar_tensor_tensor(out=PA[s][:, b, :], in0=ACC[b][:, 0:D], scalar=NSO[s][:, b:b + 1],
                                                 in1=PA[s][:, b, :], op0=ALU.mult, op1=ALU.add
                                                 ).then_inc(*dve_pre.step((s, b)))

                def residual(it, s):
                    dve.wait_ge(*act_soft.at(it, (s, 0)))
                    dve.scalar_tensor_tensor(out=PA[s], in0=PA[s], scalar=0.0, in1=XN[s][:, :, :],
                                             op0=ALU.max, op1=ALU.add).then_inc(*dve_soft.step((s, 0)))

                def add_log(it, s):
                    dve.wait_ge(*act_soft.at(it, (s, 2)))
                    dve.wait_ge(*dve_soft.at(it, (s, 0)))
                    dve.tensor_tensor(PA[s], PA[s], TMP[s], ALU.add).then_inc(*dve_soft.step((s, 1)))

                for s in SLOTS:
                    keep_xT(0, s)
                    if s == 1:
                        for half in range(2):
                            values(0, 0, half)
                    degree_in(0, s)
                    make_mask(0, s)
                    for w in range(2):
                        lo_part(0, s, 0, w)

                with dve.Fori(1, PAIRS + 1) as it:
                    for i in range(STREAM):
                        if qk_at(i - 2):
                            lo_part(it, *qk_at(i - 2))
                        if i < TILES:
                            s, g, b, j = tile_of(i)
                            if i % SEG_TILES == 0:
                                dve.wait_ge(*dve_mask.at(it, s, 1))
                            if i >= MASKED:
                                dve.wait_ge(*act_exp.at(it, i - MASKED))
                            dve.compute_val(pe_scores.at(it, i)[1])
                            dve.wait_ge(k_sem, 10)
                            dve.wait_ge(*pe_scores.at(it, i))
                            dve.tensor_tensor_reduce(
                                SM[:, i % MASKED, :], banks[4 + i % SCORE_BANKS][:, :], MASK[s][:, b, :], -float(HD) ** -0.5,
                                3.0e38, ALU.add, ALU.min, NMAX[:, i % MASKED:i % MASKED + 1]).then_inc(*dve_max.step(i))
                        if 0 <= i - 1 < 2:
                            values(it, 1, i - 1)
                        t = i - LAG
                        if 0 <= t < TILES and t % SET_TILES in BY_VECTOR:
                            dve.wait_ge(*pe_pT.at(it, t))
                            _, _, b, j = tile_of(t)
                            if t < SET_TILES and j >= 2:
                                dve.wait_ge(*spilled[j - 2].at(it, (1, 0), 1))
                            dve.tensor_copy(PT[:, t // SET_TILES % 2, j, :, b % 2 * P:(b % 2 + 1) * P],
                                            work_bank(("pT", t))[:, :].rearrange("p (k q) -> p k q", q=P)
                                            ).then_inc(*dve_pT.step(t))
                        if (p := set_at(i, 9)) is not None:
                            dve.wait_ge(*act_exp.at(it, SET_TILES * p + SET_TILES - 1))
                            dve.reciprocal(RR[:, :], RS[:, p % 2, :]).then_inc(*dve_recip.step((p, 0)))
                            dve.wait_ge(*dve_recip.at(it, (p, 0)))
                            if p >= 2:
                                dve.wait_ge(*pe_rb.at(it, p - 2))
                            dve.tensor_copy(REXP[:, p % 2 * D:(p % 2 + 1) * D].rearrange("p (t d) -> p t d", d=HD),
                                            RR[:, :].unsqueeze(2).to_broadcast([P, SET_TILES, HD])
                                            ).then_inc(*dve_recip.step((p, 1)))
                        if (p := attn_at(i)) is not None:
                            s, g, _, _ = tile_of(SET_TILES * p)
                            cols = slice(p % 2 * D, (p % 2 + 1) * D)
                            dve.wait_ge(*act_rb.at(it, p))
                            dve.wait_ge(*pe_av.at(it, p))
                            dve.tensor_tensor(AG[s][:, g, cols], OUT_T[:, cols], RBS[:, cols],
                                              ALU.mult).then_inc(*dve_attn.step(p))
                        if i - 1 in WO_AT:
                            add_attention(it, *WO_AT[i - 1])
                        if i == TILES - 1:
                            statistics(it, 0, 0)
                        if i == TILES + 2:
                            normalise(it, 0, 0)
                        if i == TILES + 3:
                            x_lo(it, 0, 0)

                    add_attention(it, 1, 0)
                    for c in range(DC):
                        sums(it, 1, 0, c)
                    add_attention(it, 1, 1)
                    statistics(it, 0, 1)
                    normalise(it, 0, 1)
                    x_lo(it, 0, 1)
                    for c in range(DC):
                        sums(it, 1, 1, c)
                    add_rows(it, 1, 0)
                    statistics(it, 1, 0)
                    normalise(it, 1, 0)
                    x_lo(it, 1, 0)
                    add_rows(it, 1, 1)
                    statistics(it, 1, 1)
                    sums(it, 2, 0, 0)
                    normalise(it, 1, 1)
                    sums(it, 2, 0, 1)
                    x_lo(it, 1, 1)
                    gram_terms(it, 0)
                    scaled_hidden(it, 0, 0)
                    for c in range(DC):
                        sums(it, 2, 1, c)
                    gram_terms(it, 1)
                    for k in range(1, HIDDEN[2]):
                        scaled_hidden(it, 0, k)
                        if k in (4, 6):
                            degree_in(it, (k - 4) // 2)
                    add_rows(it, 2, 0)
                    for k in range(HIDDEN[2]):
                        scaled_hidden(it, 1, k)
                        if k == 1:
                            statistics(it, 2, 0)
                        if k == 2:
                            normalise(it, 2, 0)
                        if k == 3:
                            statistics(it, 3, 0)
                        if k == 4:
                            normalise(it, 3, 0)
                    keep_xnT(it, 0)
                    add_rows(it, 2, 1)
                    statistics(it, 2, 1)
                    y_lo(it, 0, 0)
                    y_lo(it, 0, 1)
                    normalise(it, 2, 1)
                    y_lo(it, 0, 2)
                    statistics(it, 3, 1)
                    y_lo(it, 0, 3)
                    keep_xT(it, 0)
                    normalise(it, 3, 1)
                    keep_xnT(it, 1)
                    pre_activation(it, 0)
                    make_mask(it, 0)
                    for b in range(NB):
                        y_lo(it, 1, b)
                    residual(it, 0)
                    for w in range(2):
                        lo_part(it, 0, 0, w)
                    pre_activation(it, 1)
                    keep_xT(it, 1)
                    values(it, 0, 0)
                    statistics(it, 4, 0)
                    values(it, 0, 1)
                    residual(it, 1)
                    make_mask(it, 1)
                    lo_part(it, 1, 0, 0)
                    add_log(it, 1)
                    lo_part(it, 1, 0, 1)
                    statistics(it, 4, 1)

            @block.gpsimd
            def _(pool):
                def bias(it, L, s):
                    if L == 0:
                        for c in range(DC):
                            pool.wait_ge(*pe_xT.at(it, (s, c)))
                        src = RES[s]
                    else:
                        pool.wait_ge(*dve_norm.at(it, (L - 1, s, NB - 1)))
                        src = XN[s]
                    pool.tensor_tensor(RES[s][:, :, :], src[:, :, :], b_rows[L][:, :].unsqueeze(1).to_broadcast([P, NB, D]),
                                       ALU.add).then_inc(*pool_res.step((L, s)))

                def rstd(it, L, s):
                    pool.compute_val(dve_aggr.at(it, (L, s, NB - 1))[1])
                    pool.wait_ge(i_sem, 4)
                    pool.wait_ge(*dve_aggr.at(it, (L, s, NB - 1)))
                    pool.tensor_scalar(VE[s][:, :], MV[s][:, :, 1], LN_EPS, None, ALU.add).then_inc(*pool_var.step((L, s)))
                    pool.wait_ge(*pool_var.at(it, (L, s)))
                    pool.tensor_tensor(RSTD[s][:, :], VE[s][:, :], neg_half[:, 0:NB], ALU.pow).then_inc(*pool_rstd.step((L, s)))

                def degrees(it, s):
                    pool.wait_ge(*dve_pre.at(it, (s, NB - 1)))
                    pool.wait_ge(*act_adjT.at(it, (s, NB - 1)))
                    pool.compute_val(dve_din.at(it, s)[1])
                    pool.wait_ge(i_sem, 4)
                    pool.wait_ge(*dve_din.at(it, s))
                    pool.tensor_scalar(DNZ[s][:, :, :], DEG[s][:, :, :], 0.0, None, ALU.is_equal).then_inc(*pool_deg.step((s, 0)))
                    pool.wait_ge(*pool_deg.at(it, (s, 0)))
                    pool.tensor_tensor(DSC[s][:, :, :], DEG[s][:, :, :], DNZ[s][:, :, :], ALU.add).then_inc(*pool_deg.step((s, 1)))
                    pool.compute_val(pool_deg.at(it, (s, 1))[1])
                    pool.wait_ge(i_sem, 4)
                    pool.wait_ge(*pool_deg.at(it, (s, 1)))
                    pool.tensor_scalar(DNZ[s][:, :, :], DNZ[s][:, :, :], -1.0, 1.0, ALU.mult, ALU.add).then_inc(*pool_deg.step((s, 2)))
                    pool.tensor_tensor(DSC[s][:, :, :], DSC[s][:, :, :], neg_half[:, :].rearrange("p (a b) -> p a b", a=2),
                                       ALU.pow).then_inc(*pool_deg.step((s, 3)))
                    pool.wait_ge(*pool_deg.at(it, (s, 3)))
                    pool.tensor_tensor(DRS[s][:, :, :], DSC[s][:, :, :], DNZ[s][:, :, :], ALU.mult).then_inc(*pool_deg.step((s, 4)))
                    pool.compute_val(pool_deg.at(it, (s, 4))[1])
                    pool.wait_ge(i_sem, 4)
                    pool.wait_ge(*pool_deg.at(it, (s, 4)))
                    pool.tensor_scalar(NSO[s][:, :], DRS[s][:, 0, :], -1.0, None, ALU.mult).then_inc(*pool_deg.step((s, 5)))

                def add_log(it, s):
                    pool.wait_ge(*act_soft.at(it, (s, 2)))
                    pool.wait_ge(*dve_soft.at(it, (s, 0)))
                    pool.tensor_tensor(PA[s], PA[s], TMP[s], ALU.add).then_inc(*pool_sum.step(s))

                def normalise_out(it, s):
                    pool.compute_val(pool_rstd.at(it, (4, s))[1])
                    pool.wait_ge(i_sem, 4)
                    pool.wait_ge(*pool_rstd.at(it, (4, s)))
                    for b in range(NB):
                        pool.tensor_scalar(XN[s][:, b, :], PA[s][:, b, :], MV[s][:, b, 0:1], RSTD[s][:, b:b + 1],
                                           ALU.subtract, ALU.mult).then_inc(*pool_out.step((s, b)))

                for s in SLOTS:
                    bias(0, 0, s)
                    degrees(0, s)

                with pool.Fori(1, PAIRS + 1) as it:
                    rstd(it, 0, 0)
                    rstd(it, 0, 1)
                    bias(it, 1, 0)
                    bias(it, 1, 1)
                    rstd(it, 1, 0)
                    bias(it, 2, 0)
                    rstd(it, 1, 1)
                    bias(it, 2, 1)
                    rstd(it, 2, 0)
                    rstd(it, 3, 0)
                    rstd(it, 2, 1)
                    rstd(it, 3, 1)
                    bias(it, 0, 0)
                    degrees(it, 0)
                    add_log(it, 0)
                    bias(it, 0, 1)
                    rstd(it, 4, 0)
                    normalise_out(it, 0)
                    degrees(it, 1)
                    rstd(it, 4, 1)
                    normalise_out(it, 1)


_INS = ['x', 'adj', 'L0_gnn_Wq', 'L0_gnn_bq', 'L0_gnn_Wk', 'L0_gnn_bk', 'L0_gnn_Wv', 'L0_gnn_bv', 'L0_gnn_Wo',
        'L0_gnn_bo', 'L1_gnn_eps', 'L1_gnn_W1', 'L1_gnn_b1', 'L1_gnn_W2', 'L1_gnn_b2', 'L2_gnn_epsilon',
        'L2_gnn_W1', 'L2_gnn_b1', 'L2_gnn_rms_weight', 'L2_gnn_W2', 'L2_gnn_b2', 'L3_gnn_gamma', 'L3_gnn_beta',
        'L3_gnn_W_self', 'L3_gnn_W_neigh']


def kernel(**inputs):
    import numpy as _np
    import concourse.bacc as _bacc
    from concourse import mybir as _mybir
    from concourse.bass_utils import run_bass_kernel_spmd as _run

    nc = _bacc.Bacc("TRN2", target_bir_lowering=False, num_devices=1)
    arrays, args = {}, []
    for name in _INS:
        a = _np.ascontiguousarray(inputs[name])
        if a.ndim == 0:
            a = a.reshape(1)
        arrays[f"in_{name}"] = a
        args.append(nc.dram_tensor(f"in_{name}", a.shape, _mybir.dt.from_np(a.dtype), kind="ExternalInput").ap())
    args.append(nc.dram_tensor("out", (N_GRAPHS, N, D), F32, kind="ExternalOutput").ap())
    build(nc, *args)
    r = _run(nc, [arrays], core_ids=[0])
    return r.results[0]["out"]
```
